# Optimizing a Trainium2 kernel written in Bass

```python
import numpy as np
import jax
import jax.numpy as jnp

def _softmax(x, axis=-1):
    return jax.nn.softmax(x, axis=axis)

def _gelu(x):
    return jax.nn.gelu(x, approximate=True)

def _silu(x):
    return jax.nn.silu(x)

def _sigmoid(x):
    return jax.nn.sigmoid(x)

def _layernorm(x, axis=-1, eps=1e-05):
    m = jnp.mean(x, axis=axis, keepdims=True)
    v = jnp.var(x, axis=axis, keepdims=True)
    return (x - m) / jnp.sqrt(v + eps)

def _scatter_add(tgt, idx, src, axis=0):
    return tgt.at[idx].add(src)

def _segment_sum(src, seg, n):
    return jax.ops.segment_sum(src, seg, n)
kernel_name = 'mk_adj_preln_d2_adj_r2_157196'

def setup_inputs(seed: int=0):
    np.random.seed(seed)
    _w = jnp.asarray

    def _rec_inputs():
        import jax
        import jax.numpy as jnp
        _gk = jax.random.key(seed)
        x = -0.0005207 + 1.001 * jax.random.normal(jax.random.fold_in(_gk, 1), (8192, 128), jnp.float32)
        _a = jax.random.bernoulli(jax.random.fold_in(_gk, 2), 0.000488281, (8192, 8192))
        adj = _a.astype(jnp.int32)
        return (x, adj)
    x, adj = _rec_inputs()

    def _L0_gnn_setup():
        import jax, jax.numpy as jnp
        import numpy as np
        N = 4096
        D = 128
        NEG_SLOPE = 0.01
        MASK_VAL = -1000000000000.0
        key = jax.random.key(seed)
        k1, k2, k3, k4 = jax.random.split(key, 4)
        x = jax.random.normal(k1, (N, D), dtype=jnp.float32)
        adj = jax.random.randint(k2, (N, N), 0, 2, dtype=jnp.int32)
        W = jax.random.normal(k3, (D, D), dtype=jnp.float32) * (1.0 / np.sqrt(D))
        a = jax.random.normal(k4, (2 * D, 1), dtype=jnp.float32) * (1.0 / np.sqrt(2 * D))
        return {'x': x, 'adj': adj, 'W': W, 'a': a}
    _L0_gnn_all = _L0_gnn_setup()
    _L0_gnn_in = {k: v for k, v in _L0_gnn_all.items() if k in ('W', 'a')}
    del _L0_gnn_all

    def _L1_gnn_setup():
        import jax, jax.numpy as jnp
        import numpy as np
        N, D, H = (4096, 128, 128)
        KEEP_RATIO = 0.5
        TEMP = 1.0
        COS_EPS = 0.0001
        NEG = -9000000000000000.0

        def _cos_normalize(x):
            n = jnp.linalg.norm(x, axis=-1, keepdims=True)
            return x / jnp.maximum(n, COS_EPS)
        key = jax.random.key(seed)
        k1, k2, k3, k4 = jax.random.split(key, 4)
        features = jax.random.normal(k1, (N, D), dtype=jnp.float32)
        adj = jax.random.randint(k2, (N, N), 0, 2, dtype=jnp.int32)
        Wq = jax.random.normal(k3, (H, D), dtype=jnp.float32) * 0.001
        Wk = jax.random.normal(k4, (H, D), dtype=jnp.float32) * 0.001
        return {'features': features, 'adj': adj, 'Wq': Wq, 'Wk': Wk}
    _L1_gnn_all = _L1_gnn_setup()
    _L1_gnn_in = {k: v for k, v in _L1_gnn_all.items() if k in ('Wq', 'Wk')}
    del _L1_gnn_all
    return {'x': x, 'adj': adj, 'L0_gnn_W': _L0_gnn_in['W'], 'L0_gnn_a': _L0_gnn_in['a'], 'L1_gnn_Wq': _L1_gnn_in['Wq'], 'L1_gnn_Wk': _L1_gnn_in['Wk']}

def reference(x, adj, L0_gnn_W, L0_gnn_a, L1_gnn_Wq, L1_gnn_Wk):
    import jax
    import jax.numpy as jnp

    def _L0_gnn_ref(x, adj, W, a):
        import jax, jax.numpy as jnp
        import numpy as np
        N = 4096
        D = 128
        NEG_SLOPE = 0.01
        MASK_VAL = -1000000000000.0
        h = x @ W
        e_src = h @ a[:D, 0]
        e_dst = h @ a[D:, 0]
        e = e_src[:, None] + e_dst[None, :]
        e = jnp.where(e > 0, e, NEG_SLOPE * e)
        att_logits = jnp.where(adj > 0, e, MASK_VAL)
        attention = jax.nn.softmax(att_logits, axis=1)
        h_prime = attention @ h
        return jax.nn.elu(h_prime)

    def _L1_gnn_ref(features, adj, Wq, Wk):
        import jax, jax.numpy as jnp
        import numpy as np
        N, D, H = (4096, 128, 128)
        KEEP_RATIO = 0.5
        TEMP = 1.0
        COS_EPS = 0.0001
        NEG = -9000000000000000.0

        def _cos_normalize(x):
            n = jnp.linalg.norm(x, axis=-1, keepdims=True)
            return x / jnp.maximum(n, COS_EPS)
        Qn = _cos_normalize(features @ Wq.T)
        Kn = _cos_normalize(features @ Wk.T)
        raw_att = Kn @ Qn.T
        att = jnp.where(adj > 0, raw_att, NEG) * TEMP
        att = jax.nn.softmax(att, axis=1)
        prop_fea = att @ features
        adj_mask = (jnp.sum(adj, axis=1) > 0).astype(features.dtype)[:, None]
        prop_fea = adj_mask * prop_fea + (1.0 - adj_mask) * features
        return (1.0 - KEEP_RATIO) * prop_fea + KEEP_RATIO * features
    h = jnp.maximum(_layernorm(x, axis=-1), 0.0)
    x = x + _L0_gnn_ref(h, adj, L0_gnn_W, L0_gnn_a)
    h = jnp.maximum(_layernorm(x, axis=-1), 0.0)
    x = x + _L1_gnn_ref(h, adj, L1_gnn_Wq, L1_gnn_Wk)
    return x

_drawn_inputs = setup_inputs


def setup_inputs(seed=0):
    import zlib

    import numpy as np

    out = dict(_drawn_inputs(seed))
    spreads = {}
    factors = {}
    for name, (base, spread) in spreads.items():
        noise = np.random.default_rng([zlib.crc32(name.encode()), seed]).standard_normal(out[name].shape)
        drawn = base * np.exp(spread * noise) if base else spread * noise
        out[name] = jnp.asarray(drawn.astype(out[name].dtype))
    for name, factor in factors.items():
        out[name] = (out[name] * factor).astype(out[name].dtype)
    return out
```

```python
from contextlib import ExitStack

import numpy as np
import concourse.bass as bass
from concourse import mybir

N = 8192
D = 128
P = 128
T = N // P
ROW = 132
GROUP = 4
CB = 512
NB = N // CB
LN_EPS = 1e-5
COS_EPS = 1e-4
SLOPE = 0.01
MASKED0 = 1e12
MASKED1 = 9e15

F32 = mybir.dt.float32
I32 = mybir.dt.int32
ALU = mybir.AluOpType
ACT = mybir.ActivationFunctionType
AX = mybir.AxisListType


class Chain:

    def __init__(self, engine, done):
        self.engine, self.done, self.count, self.links = engine, done, 0, 0

    def link(self, instruction):
        self.count = self.count + 1
        self.links += 1
        instruction.then_inc(self.done, 1)
        self.engine.wait_ge(self.done, self.count)
        if not isinstance(self.count, int):
            self.engine.nop(nofuse=True)

    def repeated(self, turn, before, each):
        self.count = turn * each + before
        self.links, self.each = 0, each


def build(nc, x, adj, w0, a0, wq, wk, out):
    ctx = ExitStack()
    with ctx:
        def sb(name, shape, dt=F32):
            return ctx.enter_context(nc.sbuf_tensor(name, shape, dt))

        def sem(name):
            return ctx.enter_context(nc.semaphore(name))

        def dram(name, shape):
            return nc.dram_tensor(name, shape, F32, kind="Internal").ap()

        table0 = dram("table0", (N, ROW))
        table1 = dram("table1", (N, ROW))
        dst_row = dram("dst_row", (T, P))
        qn_cols = dram("qn_cols", (P, N))
        kn_cols = dram("kn_cols", (P, N))

        X = sb("X", [P, T, D])
        H = sb("H", [P, T, D])
        wide_a = sb("wide_a", [P, N], I32)
        wide_b = sb("wide_b", [P, N])
        w0_sb = sb("w0_sb", [P, D])
        w0T = sb("w0T", [P, D])
        a_sb = sb("a_sb", [P, 2])
        wa_sb = sb("wa_sb", [P, 2])
        wq_sb = sb("wq_sb", [P, D])
        wk_sb = sb("wk_sb", [P, D])
        wqk = sb("wqk", [P, 3, D])
        ident = sb("ident", [P, P])
        ones = sb("ones", [P, P])
        minus_half = sb("minus_half", [P, GROUP])
        stats = sb("stats", [P, 2, GROUP, 6])
        mv = sb("mv", [P, 2, GROUP, 2])
        ve = sb("ve", [P, 2, GROUP])
        rstd = sb("rstd", [P, 2, GROUP])
        nmr = sb("nmr", [P, 2, GROUP])
        h0 = sb("h0", [P, 2, GROUP, D])
        h0T = sb("h0T", [P, 2, GROUP * D])
        stage = sb("stage", [P, 2, GROUP, ROW])
        src = sb("src", [P, T])
        dst = sb("dst", [P, T])
        dstT = sb("dstT", [T, P])
        kn_t = sb("kn_t", [P, P])
        qn_b = sb("qn_b", [P, CB])
        p_b = sb("p_b", [P, CB])
        pT = sb("pT", [P, CB])
        acc = sb("acc", [P, D])
        rmax = sb("rmax", [P, 1])
        den = sb("den", [P, 1])
        rden = sb("rden", [P, 1])
        has = sb("has", [P, 1])
        hasnt = sb("hasnt", [P, 1])
        row_a = sb("row_a", [P, D])
        row_b = sb("row_b", [P, D])
        h2 = sb("h2", [P, D])
        h2T = sb("h2T", [P, D])
        n2 = sb("n2", [P, 2])
        inv = sb("inv", [P, 2])
        qk = sb("qk", [P, 2, D])
        qkT = sb("qkT", [P, 2, D])
        st1 = sb("st1", [P, 6])
        mv1 = sb("mv1", [P, 2])
        ve1 = sb("ve1", [P, 1])
        rs1 = sb("rs1", [P, 1])
        nm1 = sb("nm1", [P, 1])

        bank = [ctx.enter_context(nc.psum_tensor(f"bank{i}", [P, 512], F32)) for i in range(8)]

        x_loaded = [sem(f"x_loaded{c}") for c in range(4)]
        w_loaded = sem("w_loaded")
        consts = sem("consts")
        wT_ready = sem("wT_ready")
        wT_copied = sem("wT_copied")
        wp_ready = sem("wp_ready")
        wp_copied = sem("wp_copied")
        dve_done = sem("dve_done")
        act_done = sem("act_done")
        var_ready = sem("var_ready")
        rstd_ready = sem("rstd_ready")
        nmr_ready = sem("nmr_ready")
        h0_ready = sem("h0_ready")
        h0_turned = sem("h0_turned")
        h0T_ready = sem("h0T_ready")
        h_ready = sem("h_ready")
        h_staged = sem("h_staged")
        d_staged = sem("d_staged")
        stored0 = [sem(f"stored0_{i}") for i in range(2)]
        g_load = sem("g_load")
        g_row = sem("g_row")
        g_store = sem("g_store")
        g_dT = sem("g_dT")
        g_dTc = sem("g_dTc")
        g_kn = sem("g_kn")
        g_qb = sem("g_qb")
        g_adj = sem("g_adj")
        g_mm = sem("g_mm")
        g_mmc = sem("g_mmc")
        g_max = sem("g_max")
        g_exp = sem("g_exp")
        g_blk = sem("g_blk")
        g_pt = sem("g_pt")
        g_ptc = sem("g_ptc")
        g_pv = sem("g_pv")
        g_acc = sem("g_acc")
        g_hp = sem("g_hp")
        g_en = sem("g_en")
        g_ve = sem("g_ve")
        g_rs = sem("g_rs")
        g_h2 = sem("g_h2")
        g_h2T = sem("g_h2T")
        g_h2Tc = sem("g_h2Tc")
        g_qk = sem("g_qk")
        g_n2 = sem("g_n2")
        g_inv = sem("g_inv")
        g_qks = sem("g_qks")
        g_qkT = sem("g_qkT")
        g_qkTc = sem("g_qkTc")
        g_sv = sem("g_sv")
        g_out = sem("g_out")

        block = ctx.enter_context(nc.Block())

        xv = x.rearrange("(t p) d -> p t d", p=P)
        outv = out.rearrange("(t p) d -> t p d", p=P)
        adjv = adj.rearrange("(t p) n -> t p n", p=P)
        table0v = table0.rearrange("(t p) c -> p t c", p=P)
        table1v = table1.rearrange("(t p) c -> p t c", p=P)
        table1t = table1.rearrange("(t p) c -> t p c", p=P)
        GROUPS = T // GROUP
        CHUNK = T // 4

        def pairs(eng, first, last, step):
            with eng.Fori(0, (last - first) // 2, 1) as i:
                step(i * 2 + first, first % 2)
                step(i * 2 + (first + 1), (first + 1) % 2)

        def general_sync(sp):
            sp.wait_ge(g_dTc, 1)
            sp.nop(nofuse=True)
            sp.dma_start(dst_row, dstT[:]).then_inc(g_row, 16)
            sp.wait_ge(g_row, 16)
            sp.nop(nofuse=True)
            for layer in range(2):
                sp.dma_start(H[:], (table0v, table1v)[layer][:, :, 0:D]).then_inc(g_load, 16)
                with sp.Fori(0, T, 1) as t:
                    n = t + layer * T
                    with sp.If(n > 0):
                        sp.wait_ge(g_acc, n * NB)
                        sp.nop(nofuse=True)
                    sp.dma_start(wide_a[:], adjv[t]).then_inc(g_adj, 16)
                    if layer == 0:
                        sp.dma_start(wide_b[:], dst_row.rearrange("(o t) p -> o (t p)", o=1)
                                     .broadcast_to([P, N])).then_inc(g_kn, 16)
                        sp.wait_ge(g_h2, t + 1)
                        sp.nop(nofuse=True)
                        sp.dma_start(table1t[t][:, 0:D], h2[:]).then_inc(g_sv, 16)
                        sp.wait_ge(g_qkTc, t + 1)
                        sp.nop(nofuse=True)
                        sp.dma_start(qn_cols[:, bass.ds(t * P, P)], qkT[:, 0, :]).then_inc(g_sv, 16)
                        sp.dma_start(kn_cols[:, bass.ds(t * P, P)], qkT[:, 1, :]).then_inc(g_sv, 16)
                        sp.wait_ge(g_sv, t * 48 + 48)
                        sp.nop(nofuse=True)
                    else:
                        sp.dma_start(kn_t[:], kn_cols[:, bass.ds(t * P, P)]).then_inc(g_kn, 16)
                        with sp.Fori(0, NB, 1) as b:
                            with sp.If(t * NB + b > 0):
                                sp.wait_ge(g_mm, t * NB + b)
                                sp.nop(nofuse=True)
                            sp.dma_start(qn_b[:], qn_cols[:, bass.ds(b * CB, CB)]).then_inc(g_qb, 16)
                        sp.wait_ge(g_out, t + 1)
                        sp.nop(nofuse=True)
                        sp.dma_start(outv[t], row_a[:]).then_inc(g_store, 16)
                        sp.wait_ge(g_store, t * 16 + 16)
                        sp.nop(nofuse=True)

        def general_gpsimd(pool):
            with pool.Fori(0, T, 1) as t:
                pool.wait_ge(g_ve, t + 1)
                pool.nop(nofuse=True)
                nc.gpsimd.tensor_tensor(rs1[:], ve1[:], minus_half[:, 0:1], ALU.pow).then_inc(g_rs, 1)
                pool.wait_ge(g_n2, t + 1)
                pool.nop(nofuse=True)
                nc.gpsimd.tensor_tensor(inv[:], n2[:], minus_half[:, 0:2], ALU.pow).then_inc(g_inv, 1)

        def general_scalar(act):
            for layer in range(2):
                with act.Fori(0, T, 1) as t:
                    n = t + layer * T
                    act.wait_ge(g_max, n + 1)
                    act.nop(nofuse=True)
                    nc.scalar.activation(wide_b[:], wide_b[:], ACT.Exp, bias=rmax[:],
                                         accum_out=den[:]).then_inc(g_exp, 1)
                    act.wait_ge(g_exp, n + 1)
                    act.nop(nofuse=True)
                    with act.Fori(0, NB, 1) as b:
                        with act.If(t * NB + b + layer * T * NB > 0):
                            act.wait_ge(g_pt, t * NB + b + layer * T * NB)
                            act.nop(nofuse=True)
                        nc.scalar.activation(p_b[:], wide_b[:, bass.ds(b * CB, CB)], ACT.Copy) \
                            .then_inc(g_blk, 1)
                    if layer == 0:
                        act.wait_ge(g_hp, t + 1)
                        act.nop(nofuse=True)
                        nc.scalar.activation(row_b[:], row_b[:], ACT.Exp).then_inc(g_en, 1)
                        act.wait_ge(g_rs, t + 1)
                        act.nop(nofuse=True)
                        act.wait_ge(nmr_ready, GROUPS + t + 1)
                        act.nop(nofuse=True)
                        nc.scalar.activation(h2[:], X[:, t, :], ACT.Relu, bias=nm1[:],
                                             scale=rs1[:]).then_inc(g_h2, 1)

        def general_tensor(pe):
            pe.wait_ge(d_staged, GROUPS)
            pe.nop(nofuse=True)
            nc.tensor.transpose(bank[0][0:T, 0:P], dst[:], ident[:]).then_inc(g_dT, 1)
            pe.wait_ge(g_dTc, 1)
            pe.nop(nofuse=True)
            for layer in range(2):
                pe.wait_ge(g_load, 16 * layer + 16)
                pe.nop(nofuse=True)
                with pe.Fori(0, T, 1) as t:
                    n = t + layer * T
                    if layer == 1:
                        pe.wait_ge(g_kn, 16 * T + 16 * t + 16)
                        pe.nop(nofuse=True)
                        with pe.Fori(0, NB, 1) as b:
                            pe.wait_ge(g_qb, t * (16 * NB) + b * 16 + 16)
                            pe.nop(nofuse=True)
                            with pe.If(t * NB + b > 0):
                                pe.wait_ge(g_mmc, t * NB + b)
                                pe.nop(nofuse=True)
                            nc.tensor.matmul(bank[0][:], kn_t[:], qn_b[:], start=True, stop=True) \
                                .then_inc(g_mm, 1)
                    with pe.Fori(0, NB, 1) as b:
                        m = t * NB + b + layer * T * NB
                        pe.wait_ge(g_blk, m + 1)
                        pe.nop(nofuse=True)
                        for k in range(4):
                            last = nc.tensor.transpose(bank[1][:, k * P:(k + 1) * P],
                                                       p_b[:, k * P:(k + 1) * P], ident[:])
                        last.then_inc(g_pt, 1)
                        pe.wait_ge(g_ptc, m + 1)
                        pe.nop(nofuse=True)
                        for k in range(4):
                            last = nc.tensor.matmul(bank[2][:, 0:D], pT[:, k * P:(k + 1) * P],
                                                    H[:, b * 4 + k, :], start=(k == 0), stop=(k == 3))
                        last.then_inc(g_pv, 1)
                        pe.wait_ge(g_acc, m + 1)
                        pe.nop(nofuse=True)
                    if layer == 0:
                        pe.wait_ge(g_h2, t + 1)
                        pe.nop(nofuse=True)
                        nc.tensor.transpose(bank[3][:, 0:D], h2[:], ident[:]).then_inc(g_h2T, 1)
                        pe.wait_ge(g_h2Tc, t + 1)
                        pe.nop(nofuse=True)
                        nc.tensor.matmul(bank[3][:, 0:2 * D], h2T[:],
                                         wqk[:, 0:2, :].rearrange("p a d -> p (a d)"),
                                         start=True, stop=True).then_inc(g_qk, 1)
                        pe.wait_ge(g_qks, t + 1)
                        pe.nop(nofuse=True)
                        nc.tensor.transpose(bank[4][:, 0:D], qk[:, 0], ident[:])
                        nc.tensor.transpose(bank[4][:, D:2 * D], qk[:, 1], ident[:]).then_inc(g_qkT, 1)

        def general_vector(dve, chain):
            link = chain.link
            dve.wait_ge(g_dT, 1)
            dve.nop(nofuse=True)
            nc.vector.tensor_copy(dstT[:], bank[0][0:T, 0:P]).then_inc(g_dTc, 1)
            mask = wide_a[:].bitcast(F32)
            for layer in range(2):
                start = chain.count
                LINKS = (18, 11)[layer]
                with dve.Fori(0, T, 1) as t:
                    n = t + layer * T
                    chain.repeated(t, start, LINKS)
                    dve.wait_ge(g_adj, n * 16 + 16)
                    dve.nop(nofuse=True)
                    if layer == 0:
                        dve.wait_ge(g_kn, t * 16 + 16)
                        dve.nop(nofuse=True)
                        link(nc.vector.tensor_scalar(wide_b[:], wide_b[:], src[:, bass.ds(t, 1)], None,
                                                     ALU.add))
                        link(nc.vector.scalar_tensor_tensor(wide_b[:], wide_b[:], SLOPE, wide_b[:],
                                                            ALU.mult, ALU.max))
                    else:
                        with dve.Fori(0, NB, 1) as b:
                            dve.wait_ge(g_mm, t * NB + b + 1)
                            dve.nop(nofuse=True)
                            nc.vector.tensor_copy(wide_b[:, bass.ds(b * CB, CB)], bank[0][:]) \
                                .then_inc(g_mmc, 1)
                        dve.wait_ge(g_mmc, t * NB + NB)
                        dve.nop(nofuse=True)
                        link(nc.vector.reduce_sum(has[:], wide_a[:], AX.X))
                        link(nc.vector.tensor_scalar(has[:], has[:], 0.0, None, ALU.is_gt))
                        link(nc.vector.tensor_scalar(hasnt[:], has[:], -1.0, 1.0, ALU.mult, ALU.add))
                    big = (MASKED0, MASKED1)[layer]
                    link(nc.vector.tensor_scalar(mask, wide_a[:], 0.0, None, ALU.is_gt))
                    link(nc.vector.tensor_tensor(wide_b[:], wide_b[:], mask, ALU.mult))
                    link(nc.vector.tensor_scalar(mask, mask, -1.0, big, ALU.add, ALU.mult))
                    link(nc.vector.tensor_tensor(wide_b[:], wide_b[:], mask, ALU.add))
                    nc.vector.tensor_reduce(rmax[:], wide_b[:], AX.X, ALU.max, negate=True) \
                        .then_inc(g_max, 1)
                    dve.wait_ge(g_exp, n + 1)
                    dve.nop(nofuse=True)
                    link(nc.vector.reciprocal(rden[:], den[:]))
                    link(nc.vector.memset(acc[:], 0.0))
                    with dve.Fori(0, NB, 1) as b:
                        m = t * NB + b + layer * T * NB
                        dve.wait_ge(g_pt, m + 1)
                        dve.nop(nofuse=True)
                        nc.vector.tensor_copy(pT[:], bank[1][:]).then_inc(g_ptc, 1)
                        dve.wait_ge(g_pv, m + 1)
                        dve.nop(nofuse=True)
                        nc.vector.tensor_tensor(acc[:], acc[:], bank[2][:, 0:D], ALU.add) \
                            .then_inc(g_acc, 1)
                        dve.wait_ge(g_acc, m + 1)
                        dve.nop(nofuse=True)
                    link(nc.vector.tensor_scalar(acc[:], acc[:], rden[:], None, ALU.mult))
                    if layer == 0:
                        nc.vector.tensor_scalar(row_b[:], acc[:], 0.0, None, ALU.min).then_inc(g_hp, 1)
                        link(nc.vector.scalar_tensor_tensor(acc[:], acc[:], 0.0, X[:, t, :],
                                                            ALU.max, ALU.add))
                        dve.wait_ge(g_en, t + 1)
                        dve.nop(nofuse=True)
                        link(nc.vector.scalar_tensor_tensor(X[:, t, :], row_b[:], -1.0, acc[:],
                                                            ALU.add, ALU.add))
                        link(nc.vector.bn_stats(st1[:], X[:, t, :]))
                        link(nc.vector.bn_aggr(mv1[:], st1[:]))
                        nc.vector.tensor_scalar(ve1[:], mv1[:, 1:2], LN_EPS, None, ALU.add) \
                            .then_inc(g_ve, 1)
                        dve.wait_ge(g_rs, t + 1)
                        dve.nop(nofuse=True)
                        nc.vector.scalar_tensor_tensor(nm1[:], mv1[:, 0:1], -1.0, rs1[:],
                                                       ALU.mult, ALU.mult).then_inc(nmr_ready, 1)
                        dve.wait_ge(g_h2T, t + 1)
                        dve.nop(nofuse=True)
                        nc.vector.tensor_copy(h2T[:], bank[3][:, 0:D]).then_inc(g_h2Tc, 1)
                        dve.wait_ge(g_qk, t + 1)
                        dve.nop(nofuse=True)
                        flat = qk[:].rearrange("p a d -> p (a d)")
                        link(nc.vector.tensor_copy(flat, bank[3][:, 0:2 * D]))
                        link(nc.vector.tensor_tensor(row_a[:], qk[:, 0], qk[:, 0], ALU.mult))
                        link(nc.vector.reduce_sum(n2[:, 0:1], row_a[:], AX.X))
                        link(nc.vector.tensor_tensor(row_a[:], qk[:, 1], qk[:, 1], ALU.mult))
                        link(nc.vector.reduce_sum(n2[:, 1:2], row_a[:], AX.X))
                        nc.vector.tensor_scalar(n2[:], n2[:], COS_EPS * COS_EPS, None, ALU.max) \
                            .then_inc(g_n2, 1)
                        dve.wait_ge(g_inv, t + 1)
                        dve.nop(nofuse=True)
                        nc.vector.tensor_scalar(qk[:, 0], qk[:, 0], inv[:, 0:1], None, ALU.mult)
                        nc.vector.tensor_scalar(qk[:, 1], qk[:, 1], inv[:, 1:2], None, ALU.mult) \
                            .then_inc(g_qks, 1)
                        dve.wait_ge(g_qkT, t + 1)
                        dve.nop(nofuse=True)
                        nc.vector.tensor_copy(qkT[:].rearrange("p a d -> p (a d)"), bank[4][:, 0:2 * D]) \
                            .then_inc(g_qkTc, 1)
                        dve.wait_ge(g_sv, t * 48 + 48)
                        dve.nop(nofuse=True)
                    else:
                        link(nc.vector.tensor_scalar(acc[:], acc[:], has[:], None, ALU.mult))
                        nc.vector.scalar_tensor_tensor(acc[:], H[:, t, :], hasnt[:], acc[:],
                                                       ALU.mult, ALU.add).then_inc(g_hp, 1)
                        dve.wait_ge(g_hp, T + t + 1)
                        dve.nop(nofuse=True)
                        nc.vector.tensor_tensor(acc[:], acc[:], H[:, t, :], ALU.add).then_inc(g_n2, 1)
                        dve.wait_ge(g_n2, T + t + 1)
                        dve.nop(nofuse=True)
                        with dve.If(t > 0):
                            dve.wait_ge(g_store, t * 16)
                            dve.nop(nofuse=True)
                        nc.vector.scalar_tensor_tensor(row_a[:], acc[:], 0.5, X[:, t, :],
                                                       ALU.mult, ALU.add).then_inc(g_out, 1)
                assert chain.links == LINKS, chain.links
                chain.count = start + T * LINKS

        @block.sync
        def _(sp):
            for tile, source in ((w0_sb, w0), (wq_sb, wq), (wk_sb, wk)):
                sp.dma_start(tile[:], source).then_inc(w_loaded, 16)
            for c in range(2):
                sp.dma_start(a_sb[:, c:c + 1], a0[c * D:(c + 1) * D, :]).then_inc(w_loaded, 16)
            for c in range(4):
                sp.dma_start(X[:, c * CHUNK:(c + 1) * CHUNK, :],
                             xv[:, c * CHUNK:(c + 1) * CHUNK, :]).then_inc(x_loaded[c], 16)

            def store_h(g, par):
                sp.wait_ge(h_staged, g + 1)
                sp.wait_ge(d_staged, g + 1)
                sp.dma_start(table0v[:, bass.ds(g * GROUP, GROUP), :], stage[:, par]) \
                    .then_inc(stored0[par], 16)
            pairs(sp, 0, GROUPS, store_h)
            for par in range(2):
                sp.wait_ge(stored0[par], 16 * GROUPS // 2)
            general_sync(sp)

        @block.gpsimd
        def _(pool):
            nc.gpsimd.memset(ident[:], 0.0).then_inc(consts, 1)
            nc.gpsimd.memset(ones[:], 1.0).then_inc(consts, 1)
            nc.gpsimd.memset(minus_half[:], -0.5).then_inc(consts, 1)
            nc.gpsimd.memset(stage[:], 1.0).then_inc(consts, 1)
            pool.wait_ge(consts, 4)
            nc.gpsimd.affine_select(out=ident[:], in_=ident[:], compare_op=ALU.not_equal, fill=1.0,
                                    base=0, pattern=[[-1, P]], channel_multiplier=1).then_inc(consts, 1)

            def rsqrt_var(g, par):
                pool.wait_ge(var_ready, g + 1)
                nc.gpsimd.tensor_tensor(rstd[:, par], ve[:, par], minus_half[:], ALU.pow) \
                    .then_inc(rstd_ready, 1)
            pairs(pool, 0, GROUPS, rsqrt_var)
            general_gpsimd(pool)

        @block.scalar
        def _(act):
            def norm_relu(g, par):
                act.wait_ge(nmr_ready, g + 1)
                for k in range(GROUP):
                    last = nc.scalar.activation(h0[:, par, k], X[:, g * GROUP + k, :], ACT.Relu,
                                                bias=nmr[:, par, k:k + 1], scale=rstd[:, par, k:k + 1])
                last.then_inc(h0_ready, 1)

            def stage_h(g, par):
                act.wait_ge(h_ready, g + 1)
                if isinstance(g, int) and g < 2:
                    pass
                else:
                    act.wait_ge(stored0[par], 8 * (g - par))
                nc.scalar.activation(stage[:, par, :, 0:D],
                                     bank[2 + par][:].rearrange("p (k d) -> p k d", d=D), ACT.Copy) \
                    .then_inc(h_staged, 1)

            norm_relu(0, 0)
            norm_relu(1, 1)
            act.wait_ge(consts, 5)
            stage_h(0, 0)
            norm_relu(2, 0)
            stage_h(1, 1)

            def both(g, par):
                norm_relu(g, par)
                stage_h(g - 1, 1 - par)
            pairs(act, 3, GROUPS - 1, both)
            both(GROUPS - 1, (GROUPS - 1) % 2)
            stage_h(GROUPS - 1, (GROUPS - 1) % 2)
            general_scalar(act)

        @block.tensor
        def _(pe):
            pe.wait_ge(w_loaded, 80)
            pe.wait_ge(consts, 5)
            nc.tensor.transpose(bank[4][:, 0:D], w0_sb[:], ident[:])
            nc.tensor.transpose(bank[4][:, D:2 * D], wq_sb[:], ident[:])
            nc.tensor.transpose(bank[4][:, 2 * D:3 * D], wk_sb[:], ident[:])
            nc.tensor.matmul(bank[4][:, 3 * D:4 * D], wk_sb[:], wq_sb[:], start=True, stop=True) \
                .then_inc(wT_ready, 1)
            pe.wait_ge(wT_copied, 1)
            nc.tensor.matmul(bank[5][:, 0:2], w0T[:], a_sb[:], start=True, stop=True) \
                .then_inc(wp_ready, 1)
            pe.wait_ge(wp_copied, 1)

            def turn_h0(g, par):
                pe.wait_ge(h0_ready, g + 1)
                if isinstance(g, int) and g < 2:
                    pass
                else:
                    pe.wait_ge(h0T_ready, g - 1)
                for k in range(GROUP):
                    last = nc.tensor.transpose(bank[par][:, k * D:(k + 1) * D], h0[:, par, k], ident[:])
                last.then_inc(h0_turned, 1)

            def project(g, par):
                pe.wait_ge(h0T_ready, g + 1)
                if isinstance(g, int) and g < 2:
                    pass
                else:
                    pe.wait_ge(h_staged, g - 1)
                    pe.wait_ge(d_staged, g - 1)
                for k in range(GROUP):
                    left = h0T[:, par, k * D:(k + 1) * D]
                    nc.tensor.matmul(bank[2 + par][:, k * D:(k + 1) * D], left, w0_sb[:],
                                     start=True, stop=True)
                    last = nc.tensor.matmul(bank[6 + par][:, 2 * k:2 * k + 2], left, wa_sb[:],
                                            start=True, stop=True)
                last.then_inc(h_ready, 1)

            turn_h0(0, 0)
            turn_h0(1, 1)
            project(0, 0)
            turn_h0(2, 0)
            project(1, 1)

            def both(g, par):
                turn_h0(g, par)
                project(g - 1, 1 - par)
            pairs(pe, 3, GROUPS - 1, both)
            both(GROUPS - 1, (GROUPS - 1) % 2)
            project(GROUPS - 1, (GROUPS - 1) % 2)
            general_tensor(pe)

        @block.vector
        def _(dve):
            chain = Chain(dve, dve_done)
            link = chain.link
            dve.wait_ge(wT_ready, 1)
            link(nc.vector.tensor_copy(wqk[:].rearrange("p a d -> p (a d)"), bank[4][:, D:4 * D]))
            nc.vector.tensor_copy(w0T[:], bank[4][:, 0:D]).then_inc(wT_copied, 1)
            dve.wait_ge(wp_ready, 1)
            nc.vector.tensor_copy(wa_sb[:], bank[5][:, 0:2]).then_inc(wp_copied, 1)
            FRONT = 2

            def moments(g, par):
                for k in range(GROUP):
                    last = nc.vector.bn_stats(stats[:, par, k], X[:, g * GROUP + k, :])
                link(last)
                for k in range(GROUP):
                    last = nc.vector.bn_aggr(mv[:, par, k], stats[:, par, k])
                link(last)
                nc.vector.tensor_scalar(ve[:, par], mv[:, par, :, 1], LN_EPS, None, ALU.add) \
                    .then_inc(var_ready, 1)
                dve.wait_ge(rstd_ready, g + 1)
                nc.vector.scalar_tensor_tensor(nmr[:, par], mv[:, par, :, 0], -1.0, rstd[:, par],
                                               ALU.mult, ALU.mult).then_inc(nmr_ready, 1)

            def copy_h0T(g, par):
                dve.wait_ge(h0_turned, g + 1)
                if isinstance(g, int) and g < 2:
                    pass
                else:
                    dve.wait_ge(h_ready, g - 1)
                nc.vector.tensor_copy(h0T[:, par], bank[par][:]).then_inc(h0T_ready, 1)

            def stage_d(g, par):
                dve.wait_ge(h_ready, g + 1)
                if isinstance(g, int) and g < 2:
                    pass
                else:
                    dve.wait_ge(stored0[par], 8 * (g - par))
                both = bank[6 + par][:, 0:2 * GROUP].rearrange("p (k c) -> p k c", c=2)
                nc.vector.tensor_copy(src[:, bass.ds(g * GROUP, GROUP)], both[:, :, 0])
                nc.vector.tensor_copy(dst[:, bass.ds(g * GROUP, GROUP)], both[:, :, 1])
                nc.vector.tensor_copy(stage[:, par, :, D], both[:, :, 1]).then_inc(d_staged, 1)

            for c in range(4):
                dve.wait_ge(x_loaded[c], 16)
            dve.wait_ge(consts, 5)
            moments(0, 0)
            moments(1, 1)
            copy_h0T(0, 0)
            moments(2, 0)
            copy_h0T(1, 1)
            stage_d(0, 0)
            start = chain.count - 3 * FRONT

            def step(g, par):
                chain.repeated(g, start, FRONT)
                moments(g, par)
                copy_h0T(g - 1, 1 - par)
                stage_d(g - 2, par)
            pairs(dve, 3, GROUPS - 1, step)
            step(GROUPS - 1, (GROUPS - 1) % 2)
            copy_h0T(GROUPS - 1, (GROUPS - 1) % 2)
            stage_d(GROUPS - 2, GROUPS % 2)
            stage_d(GROUPS - 1, (GROUPS - 1) % 2)
            general_vector(dve, chain)



def kernel(x, adj, L0_gnn_W, L0_gnn_a, L1_gnn_Wq, L1_gnn_Wk):
    import numpy as _np
    import concourse.bacc as _bacc
    from concourse import mybir as _mybir
    from concourse.bass_utils import run_bass_kernel_spmd as _run

    nc = _bacc.Bacc("TRN2", target_bir_lowering=False, num_devices=1)
    arrays, args = {}, []
    for name, a in (("x", x), ("adj", adj), ("w0", L0_gnn_W), ("a0", L0_gnn_a),
                    ("wq", L1_gnn_Wq), ("wk", L1_gnn_Wk)):
        a = _np.ascontiguousarray(a)
        arrays[f"in_{name}"] = a
        args.append(nc.dram_tensor(f"in_{name}", a.shape, _mybir.dt.from_np(a.dtype),
                                   kind="ExternalInput").ap())
    result = nc.dram_tensor("out_rows", (N, D), F32, kind="ExternalOutput")
    build(nc, *args, result.ap())
    r = _run(nc, [arrays], core_ids=[0])
    return r.results[0]["out_rows"]
```

```python
from contextlib import ExitStack

import numpy as np
import concourse.bass as bass
from concourse import mybir

N = 8192
D = 128
P = 128
T = N // P
ROW = 132
GROUP = 4
CB = 512
NB = N // CB
SEG = 2048
SEGS = N // SEG
WORDS = SEG // 4
HITS = 8
SLOTS = 16
CHUNKS = 5
EDGES = CHUNKS * P
BASE = 64.0
LEAST_SUM = 2.0 ** -40
TINY = 1e-30
LN_EPS = 1e-5
COS_EPS = 1e-4
SLOPE = 0.01
MASKED0 = 1e12
MASKED1 = 9e15

F32 = mybir.dt.float32
I32 = mybir.dt.int32
U32 = mybir.dt.uint32
U8 = mybir.dt.uint8
ALU = mybir.AluOpType
ACT = mybir.ActivationFunctionType
AX = mybir.AxisListType


class Chain:

    def __init__(self, engine, done):
        self.engine, self.done, self.count, self.links = engine, done, 0, 0

    def link(self, instruction):
        self.count = self.count + 1
        self.links += 1
        instruction.then_inc(self.done, 1)
        self.engine.wait_ge(self.done, self.count)
        if not isinstance(self.count, int):
            self.engine.nop(nofuse=True)

    def repeated(self, turn, before, each):
        self.count = turn * each + before
        self.links, self.each = 0, each


def build(nc, x, adj, w0, a0, wq, wk, out):
    ctx = ExitStack()
    with ctx:
        def sb(name, shape, dt=F32):
            return ctx.enter_context(nc.sbuf_tensor(name, shape, dt))

        def sem(name):
            return ctx.enter_context(nc.semaphore(name))

        def dram(name, shape):
            return nc.dram_tensor(name, shape, F32, kind="Internal").ap()

        rows0 = dram("rows0", (N + 1, ROW))
        rows1 = dram("rows1", (N + 1, ROW))
        table0, table1 = rows0[1:N + 1, :], rows1[1:N + 1, :]
        dst_row = dram("dst_row", (T, P))
        qn_cols = dram("qn_cols", (P, N))
        kn_cols = dram("kn_cols", (P, N))

        X = sb("X", [P, T, D])
        H = sb("H", [P, T, D])
        wide = sb("wide", [P, 2, N], I32)
        wide_a = wide[:, 0]
        wide_b = wide[:, 1].bitcast(F32)
        w0_sb = sb("w0_sb", [P, D])
        w0T = sb("w0T", [P, D])
        a_sb = sb("a_sb", [P, 2])
        wa_sb = sb("wa_sb", [P, 2])
        wq_sb = sb("wq_sb", [P, D])
        wk_sb = sb("wk_sb", [P, D])
        wqk = sb("wqk", [P, 3, D])
        ident = sb("ident", [P, P])
        ones = sb("ones", [P, P])
        minus_half = sb("minus_half", [P, GROUP])
        stats = sb("stats", [P, 2, GROUP, 6])
        mv = sb("mv", [P, 2, GROUP, 2])
        ve = sb("ve", [P, 2, GROUP])
        rstd = sb("rstd", [P, 2, GROUP])
        nmr = sb("nmr", [P, 2, GROUP])
        h0 = sb("h0", [P, 2, GROUP, D])
        h0T = sb("h0T", [P, 2, GROUP * D])
        stage = sb("stage", [P, 2, GROUP, ROW])
        src = sb("src", [P, T])
        dst = sb("dst", [P, T])
        dstT = sb("dstT", [T, P])
        zero_row = sb("zero_row", [1, ROW])
        tri = sb("tri", [P, P])
        lane = sb("lane", [P, P])
        edge_mid = sb("edge_mid", [P, EDGES])
        edge_no = sb("edge_no", [P, CHUNKS])
        slot_no = sb("slot_no", [P, SLOTS])
        seg_base = sb("seg_base", [P, SEGS, HITS])
        byte_base = sb("byte_base", [P, 4])
        base_bias = sb("base_bias", [P, 1])
        mean_h = sb("mean_h", [P, D])
        dst_max = sb("dst_max", [P, 1])
        dmax_p = sb("dmax_p", [P, 1])
        entries = sb("entries", [P, T, SEGS])
        count = sb("count", [P, T])
        total = sb("total", [P, T])
        least = sb("least", [P, T])
        neg_mid = sb("neg_mid", [P, T])
        reach = sb("reach", [P, T])
        edge_node = sb("edge_node", [P, T, CHUNKS], U32)
        edge_row = sb("edge_row", [P, T, CHUNKS])
        packed = sb("packed", [P, 2, SEGS, SEG], U8)
        top = sb("top", [P, 2, SEGS, HITS])
        at = sb("at", [P, 2, SEGS, HITS], U32)
        at_base = sb("at_base", [P, SEGS * HITS])
        cand_no = sb("cand_no", [P, SEGS * HITS, 4])
        cand = sb("cand", [P, SEGS * HITS * 4])
        cand_b = sb("cand_b", [P, SEGS * HITS * 4])
        used = sb("used", [P, SLOTS])
        row_info = sb("row_info", [P, 2, SLOTS + 3])
        away = sb("away", [P, 2, EDGES])
        spread = sb("spread", [P, 2, EDGES])
        nth = sb("nth", [P, CHUNKS])
        pick = sb("pick", [P, CHUNKS, SLOTS])
        picked = sb("picked", [P, CHUNKS, SLOTS])
        node_1 = sb("node_1", [P, CHUNKS])
        gather_at = sb("gather_at", [P, 2, CHUNKS], U32)
        edge_src = sb("edge_src", [P, 2, CHUNKS])
        G = sb("G", [P, 2, CHUNKS, ROW])
        z = sb("z", [P, CHUNKS])
        zm = sb("zm", [P, CHUNKS])
        lz = sb("lz", [P, CHUNKS])
        lzm = sb("lzm", [P, CHUNKS])
        lg = sb("lg", [P, CHUNKS])
        logit = sb("logit", [P, 2, CHUNKS])
        weight = sb("weight", [P, 2, CHUNKS])
        collect = sb("collect", [P, 2, CHUNKS, P])
        denc = sb("denc", [P, 1])
        rd = sb("rd", [P, 2])
        lone = sb("lone", [P, 2])
        hp = sb("hp", [P, 2, D])
        hmin = sb("hmin", [P, 2, D])
        hsum = sb("hsum", [P, D])
        half_f = sb("half_f", [P, 2])
        bad = sb("bad", [P, 3, T])
        bad_p = sb("bad_p", [P, 1])
        chk = sb("chk", [P, T])
        flag = sb("flag", [P, 1], I32)
        unread = h0[:].rearrange("p a k d -> p (a k) d")
        n2s = sb("n2s", [P, 2, 2])
        invs = sb("invs", [P, 2, 2])
        kn_t = sb("kn_t", [P, P])
        qn_b = spread[:, 0, 0:CB]
        p_b = collect[:, 0, 0:4].rearrange("p c q -> p (c q)")
        pT = collect[:, 1, 0:4].rearrange("p c q -> p (c q)")
        acc = sb("acc", [P, D])
        rmax = sb("rmax", [P, 1])
        den = sb("den", [P, 1])
        rden = sb("rden", [P, 1])
        has = sb("has", [P, 1])
        hasnt = sb("hasnt", [P, 1])
        row_a = sb("row_a", [P, D])
        row_b = sb("row_b", [P, D])
        h2 = sb("h2", [P, D])
        h2T = sb("h2T", [P, D])
        n2 = sb("n2", [P, 2])
        inv = sb("inv", [P, 2])
        qk = sb("qk", [P, 2, D])
        qkT = sb("qkT", [P, 2, D])
        st1 = sb("st1", [P, 6])
        mv1 = sb("mv1", [P, 2])
        ve1 = sb("ve1", [P, 1])
        rs1 = sb("rs1", [P, 1])
        nm1 = sb("nm1", [P, 1])

        bank = [ctx.enter_context(nc.psum_tensor(f"bank{i}", [P, 512], F32)) for i in range(8)]

        x_loaded = [sem(f"x_loaded{c}") for c in range(4)]
        w_loaded = sem("w_loaded")
        consts = sem("consts")
        wT_ready = sem("wT_ready")
        wT_copied = sem("wT_copied")
        wp_ready = sem("wp_ready")
        wp_copied = sem("wp_copied")
        dve_done = sem("dve_done")
        act_done = sem("act_done")
        var_ready = sem("var_ready")
        rstd_ready = sem("rstd_ready")
        nmr_ready = sem("nmr_ready")
        h0_ready = sem("h0_ready")
        h0_turned = sem("h0_turned")
        h0T_ready = sem("h0T_ready")
        h_ready = sem("h_ready")
        h_staged = sem("h_staged")
        d_staged = sem("d_staged")
        stored0 = [sem(f"stored0_{i}") for i in range(2)]
        zeroed = sem("zeroed")
        zero_stored = sem("zero_stored")
        sp_const = sem("sp_const")
        mean_done = sem("mean_done")
        halved = sem("halved")
        dmax_own = sem("dmax_own")
        dmax_turned = sem("dmax_turned")
        dmax_one = sem("dmax_one")
        dmax_all = sem("dmax_all")
        dmax_ready = sem("dmax_ready")
        adj_loaded = [[sem(f"adj_loaded{p}{h}") for h in range(2)] for p in range(2)]
        half_packed = sem("half_packed")
        searched = sem("searched")
        counted = sem("counted")
        summed = sem("summed")
        mid_ready = sem("mid_ready")
        away_ready = sem("away_ready")
        spread_ready = sem("spread_ready")
        spread_out = sem("spread_out")
        listed = sem("listed")
        gathered = [sem(f"gathered{p}") for p in range(2)]
        logit_ready = sem("logit_ready")
        weight_ready = sem("weight_ready")
        collect_ready = sem("collect_ready")
        collected = sem("collected")
        rd_ready = sem("rd_ready")
        hp_ready = sem("hp_ready")
        min_ready = sem("min_ready")
        exp_ready = sem("exp_ready")
        v_ready = sem("v_ready")
        r_ready = sem("r_ready")
        m_ready = sem("m_ready")
        f_ready = sem("f_ready")
        f_turned = sem("f_turned")
        fT_ready = sem("fT_ready")
        q_ready = sem("q_ready")
        norms_ready = sem("norms_ready")
        norms_kept = sem("norms_kept")
        inv_ready = sem("inv_ready")
        u_ready = sem("u_ready")
        row_staged = sem("row_staged")
        stored1 = [sem(f"stored1_{p}") for p in range(2)]
        bad_ready = sem("bad_ready")
        bad_all = sem("bad_all")
        flag_ready = sem("flag_ready")
        b_at = sem("b_at")
        b_away = sem("b_away")
        b_spread = sem("b_spread")
        b_u = sem("b_u")
        b_dot = sem("b_dot")
        b_weight = sem("b_weight")
        b_collect = sem("b_collect")
        b_sum = sem("b_sum")
        b_rd = sem("b_rd")
        b_scaled = sem("b_scaled")
        b_out = sem("b_out")
        b_stored = [sem(f"b_stored{p}") for p in range(2)]
        g_load = sem("g_load")
        g_row = sem("g_row")
        g_store = sem("g_store")
        g_dT = sem("g_dT")
        g_dTc = sem("g_dTc")
        g_kn = sem("g_kn")
        g_qb = sem("g_qb")
        g_adj = sem("g_adj")
        g_mm = sem("g_mm")
        g_mmc = sem("g_mmc")
        g_max = sem("g_max")
        g_exp = sem("g_exp")
        g_blk = sem("g_blk")
        g_pt = sem("g_pt")
        g_ptc = sem("g_ptc")
        g_pv = sem("g_pv")
        g_acc = sem("g_acc")
        g_hp = sem("g_hp")
        g_en = sem("g_en")
        g_ve = sem("g_ve")
        g_rs = sem("g_rs")
        g_h2 = sem("g_h2")
        g_h2T = sem("g_h2T")
        g_h2Tc = sem("g_h2Tc")
        g_qk = sem("g_qk")
        g_n2 = sem("g_n2")
        g_inv = sem("g_inv")
        g_qks = sem("g_qks")
        g_qkT = sem("g_qkT")
        g_qkTc = sem("g_qkTc")
        g_sv = sem("g_sv")
        g_out = sem("g_out")

        block = ctx.enter_context(nc.Block())

        xv = x.rearrange("(t p) d -> p t d", p=P)
        outv = out.rearrange("(t p) d -> t p d", p=P)
        adjv = adj.rearrange("(t p) n -> t p n", p=P)
        table0v = table0.rearrange("(t p) c -> p t c", p=P)
        table1v = table1.rearrange("(t p) c -> p t c", p=P)
        table1t = table1.rearrange("(t p) c -> t p c", p=P)
        GROUPS = T // GROUP
        CHUNK = T // 4

        def pairs(eng, first, last, step):
            with eng.Fori(0, (last - first) // 2, 1) as i:
                step(i * 2 + first, first % 2)
                step(i * 2 + (first + 1), (first + 1) % 2)

        def general_sync(sp):
            sp.wait_ge(g_dTc, 1)
            sp.nop(nofuse=True)
            sp.dma_start(dst_row, dstT[:]).then_inc(g_row, 16)
            sp.wait_ge(g_row, 16)
            sp.nop(nofuse=True)
            for layer in range(2):
                if layer == 0:
                    sp.dma_start(X[:], xv).then_inc(g_row, 16)
                    sp.wait_ge(g_row, 32)
                    sp.nop(nofuse=True)
                sp.dma_start(H[:], (table0v, table1v)[layer][:, :, 0:D]).then_inc(g_load, 16)
                with sp.Fori(0, T, 1) as t:
                    n = t + layer * T
                    with sp.If(n > 0):
                        sp.wait_ge(g_acc, n * NB)
                        sp.nop(nofuse=True)
                    sp.dma_start(wide_a, adjv[t]).then_inc(g_adj, 16)
                    if layer == 0:
                        sp.dma_start(wide_b, dst_row.rearrange("(o t) p -> o (t p)", o=1)
                                     .broadcast_to([P, N])).then_inc(g_kn, 16)
                        sp.wait_ge(g_h2, t + 1)
                        sp.nop(nofuse=True)
                        sp.dma_start(table1t[t][:, 0:D], h2[:]).then_inc(g_sv, 16)
                        sp.wait_ge(g_qkTc, t + 1)
                        sp.nop(nofuse=True)
                        sp.dma_start(qn_cols[:, bass.ds(t * P, P)], qkT[:, 0, :]).then_inc(g_sv, 16)
                        sp.dma_start(kn_cols[:, bass.ds(t * P, P)], qkT[:, 1, :]).then_inc(g_sv, 16)
                        sp.wait_ge(g_sv, t * 48 + 48)
                        sp.nop(nofuse=True)
                    else:
                        sp.dma_start(kn_t[:], kn_cols[:, bass.ds(t * P, P)]).then_inc(g_kn, 16)
                        with sp.Fori(0, NB, 1) as b:
                            with sp.If(t * NB + b > 0):
                                sp.wait_ge(g_mm, t * NB + b)
                                sp.nop(nofuse=True)
                            sp.dma_start(qn_b, qn_cols[:, bass.ds(b * CB, CB)]).then_inc(g_qb, 16)
                        sp.wait_ge(g_out, t + 1)
                        sp.nop(nofuse=True)
                        sp.dma_start(outv[t], row_a[:]).then_inc(g_store, 16)
                        sp.wait_ge(g_store, t * 16 + 16)
                        sp.nop(nofuse=True)

        def general_gpsimd(pool):
            with pool.Fori(0, T, 1) as t:
                pool.wait_ge(g_ve, t + 1)
                pool.nop(nofuse=True)
                nc.gpsimd.tensor_tensor(rs1[:], ve1[:], minus_half[:, 0:1], ALU.pow).then_inc(g_rs, 1)
                pool.wait_ge(g_n2, t + 1)
                pool.nop(nofuse=True)
                nc.gpsimd.tensor_tensor(inv[:], n2[:], minus_half[:, 0:2], ALU.pow).then_inc(g_inv, 1)

        def general_scalar(act):
            for layer in range(2):
                with act.Fori(0, T, 1) as t:
                    n = t + layer * T
                    act.wait_ge(g_max, n + 1)
                    act.nop(nofuse=True)
                    nc.scalar.activation(wide_b, wide_b, ACT.Exp, bias=rmax[:],
                                         accum_out=den[:]).then_inc(g_exp, 1)
                    act.wait_ge(g_exp, n + 1)
                    act.nop(nofuse=True)
                    with act.Fori(0, NB, 1) as b:
                        with act.If(t * NB + b + layer * T * NB > 0):
                            act.wait_ge(g_pt, t * NB + b + layer * T * NB)
                            act.nop(nofuse=True)
                        nc.scalar.activation(p_b, wide_b[:, bass.ds(b * CB, CB)], ACT.Copy) \
                            .then_inc(g_blk, 1)
                    if layer == 0:
                        act.wait_ge(g_hp, t + 1)
                        act.nop(nofuse=True)
                        nc.scalar.activation(row_b[:], row_b[:], ACT.Exp).then_inc(g_en, 1)
                        act.wait_ge(g_rs, t + 1)
                        act.nop(nofuse=True)
                        act.wait_ge(nmr_ready, GROUPS + t + 1)
                        act.nop(nofuse=True)
                        nc.scalar.activation(h2[:], X[:, t, :], ACT.Relu, bias=nm1[:],
                                             scale=rs1[:]).then_inc(g_h2, 1)

        def general_tensor(pe):
            pe.wait_ge(d_staged, GROUPS)
            pe.nop(nofuse=True)
            nc.tensor.transpose(bank[0][0:T, 0:P], dst[:], ident[:]).then_inc(g_dT, 1)
            pe.wait_ge(g_dTc, 1)
            pe.nop(nofuse=True)
            for layer in range(2):
                pe.wait_ge(g_load, 16 * layer + 16)
                pe.nop(nofuse=True)
                with pe.Fori(0, T, 1) as t:
                    n = t + layer * T
                    if layer == 1:
                        pe.wait_ge(g_kn, 16 * T + 16 * t + 16)
                        pe.nop(nofuse=True)
                        with pe.Fori(0, NB, 1) as b:
                            pe.wait_ge(g_qb, t * (16 * NB) + b * 16 + 16)
                            pe.nop(nofuse=True)
                            with pe.If(t * NB + b > 0):
                                pe.wait_ge(g_mmc, t * NB + b)
                                pe.nop(nofuse=True)
                            nc.tensor.matmul(bank[0][:], kn_t[:], qn_b, start=True, stop=True) \
                                .then_inc(g_mm, 1)
                    with pe.Fori(0, NB, 1) as b:
                        m = t * NB + b + layer * T * NB
                        pe.wait_ge(g_blk, m + 1)
                        pe.nop(nofuse=True)
                        for k in range(4):
                            last = nc.tensor.transpose(bank[1][:, k * P:(k + 1) * P],
                                                       p_b[:, k * P:(k + 1) * P], ident[:])
                        last.then_inc(g_pt, 1)
                        pe.wait_ge(g_ptc, m + 1)
                        pe.nop(nofuse=True)
                        for k in range(4):
                            last = nc.tensor.matmul(bank[2][:, 0:D], pT[:, k * P:(k + 1) * P],
                                                    H[:, b * 4 + k, :], start=(k == 0), stop=(k == 3))
                        last.then_inc(g_pv, 1)
                        pe.wait_ge(g_acc, m + 1)
                        pe.nop(nofuse=True)
                    if layer == 0:
                        pe.wait_ge(g_h2, t + 1)
                        pe.nop(nofuse=True)
                        nc.tensor.transpose(bank[3][:, 0:D], h2[:], ident[:]).then_inc(g_h2T, 1)
                        pe.wait_ge(g_h2Tc, t + 1)
                        pe.nop(nofuse=True)
                        nc.tensor.matmul(bank[3][:, 0:2 * D], h2T[:],
                                         wqk[:, 0:2, :].rearrange("p a d -> p (a d)"),
                                         start=True, stop=True).then_inc(g_qk, 1)
                        pe.wait_ge(g_qks, t + 1)
                        pe.nop(nofuse=True)
                        nc.tensor.transpose(bank[4][:, 0:D], qk[:, 0], ident[:])
                        nc.tensor.transpose(bank[4][:, D:2 * D], qk[:, 1], ident[:]).then_inc(g_qkT, 1)

        def general_vector(dve, chain):
            link = chain.link
            dve.wait_ge(g_dT, 1)
            dve.nop(nofuse=True)
            nc.vector.tensor_copy(dstT[:], bank[0][0:T, 0:P]).then_inc(g_dTc, 1)
            mask = wide_a.bitcast(F32)
            for layer in range(2):
                start = chain.count
                LINKS = (18, 11)[layer]
                with dve.Fori(0, T, 1) as t:
                    n = t + layer * T
                    chain.repeated(t, start, LINKS)
                    dve.wait_ge(g_adj, n * 16 + 16)
                    dve.nop(nofuse=True)
                    if layer == 0:
                        dve.wait_ge(g_kn, t * 16 + 16)
                        dve.nop(nofuse=True)
                        link(nc.vector.tensor_scalar(wide_b, wide_b, src[:, bass.ds(t, 1)], None,
                                                     ALU.add))
                        link(nc.vector.scalar_tensor_tensor(wide_b, wide_b, SLOPE, wide_b,
                                                            ALU.mult, ALU.max))
                    else:
                        with dve.Fori(0, NB, 1) as b:
                            dve.wait_ge(g_mm, t * NB + b + 1)
                            dve.nop(nofuse=True)
                            nc.vector.tensor_copy(wide_b[:, bass.ds(b * CB, CB)], bank[0][:]) \
                                .then_inc(g_mmc, 1)
                        dve.wait_ge(g_mmc, t * NB + NB)
                        dve.nop(nofuse=True)
                        link(nc.vector.reduce_sum(has[:], wide_a, AX.X))
                        link(nc.vector.tensor_scalar(has[:], has[:], 0.0, None, ALU.is_gt))
                        link(nc.vector.tensor_scalar(hasnt[:], has[:], -1.0, 1.0, ALU.mult, ALU.add))
                    big = (MASKED0, MASKED1)[layer]
                    link(nc.vector.tensor_scalar(mask, wide_a, 0.0, None, ALU.is_gt))
                    link(nc.vector.tensor_tensor(wide_b, wide_b, mask, ALU.mult))
                    link(nc.vector.tensor_scalar(mask, mask, -1.0, big, ALU.add, ALU.mult))
                    link(nc.vector.tensor_tensor(wide_b, wide_b, mask, ALU.add))
                    nc.vector.tensor_reduce(rmax[:], wide_b, AX.X, ALU.max, negate=True) \
                        .then_inc(g_max, 1)
                    dve.wait_ge(g_exp, n + 1)
                    dve.nop(nofuse=True)
                    link(nc.vector.reciprocal(rden[:], den[:]))
                    link(nc.vector.memset(acc[:], 0.0))
                    with dve.Fori(0, NB, 1) as b:
                        m = t * NB + b + layer * T * NB
                        dve.wait_ge(g_pt, m + 1)
                        dve.nop(nofuse=True)
                        nc.vector.tensor_copy(pT, bank[1][:]).then_inc(g_ptc, 1)
                        dve.wait_ge(g_pv, m + 1)
                        dve.nop(nofuse=True)
                        nc.vector.tensor_tensor(acc[:], acc[:], bank[2][:, 0:D], ALU.add) \
                            .then_inc(g_acc, 1)
                        dve.wait_ge(g_acc, m + 1)
                        dve.nop(nofuse=True)
                    link(nc.vector.tensor_scalar(acc[:], acc[:], rden[:], None, ALU.mult))
                    if layer == 0:
                        nc.vector.tensor_scalar(row_b[:], acc[:], 0.0, None, ALU.min).then_inc(g_hp, 1)
                        link(nc.vector.scalar_tensor_tensor(acc[:], acc[:], 0.0, X[:, t, :],
                                                            ALU.max, ALU.add))
                        dve.wait_ge(g_en, t + 1)
                        dve.nop(nofuse=True)
                        link(nc.vector.scalar_tensor_tensor(X[:, t, :], row_b[:], -1.0, acc[:],
                                                            ALU.add, ALU.add))
                        link(nc.vector.bn_stats(st1[:], X[:, t, :]))
                        link(nc.vector.bn_aggr(mv1[:], st1[:]))
                        nc.vector.tensor_scalar(ve1[:], mv1[:, 1:2], LN_EPS, None, ALU.add) \
                            .then_inc(g_ve, 1)
                        dve.wait_ge(g_rs, t + 1)
                        dve.nop(nofuse=True)
                        nc.vector.scalar_tensor_tensor(nm1[:], mv1[:, 0:1], -1.0, rs1[:],
                                                       ALU.mult, ALU.mult).then_inc(nmr_ready, 1)
                        dve.wait_ge(g_h2T, t + 1)
                        dve.nop(nofuse=True)
                        nc.vector.tensor_copy(h2T[:], bank[3][:, 0:D]).then_inc(g_h2Tc, 1)
                        dve.wait_ge(g_qk, t + 1)
                        dve.nop(nofuse=True)
                        flat = qk[:].rearrange("p a d -> p (a d)")
                        link(nc.vector.tensor_copy(flat, bank[3][:, 0:2 * D]))
                        link(nc.vector.tensor_tensor(row_a[:], qk[:, 0], qk[:, 0], ALU.mult))
                        link(nc.vector.reduce_sum(n2[:, 0:1], row_a[:], AX.X))
                        link(nc.vector.tensor_tensor(row_a[:], qk[:, 1], qk[:, 1], ALU.mult))
                        link(nc.vector.reduce_sum(n2[:, 1:2], row_a[:], AX.X))
                        nc.vector.tensor_scalar(n2[:], n2[:], COS_EPS * COS_EPS, None, ALU.max) \
                            .then_inc(g_n2, 1)
                        dve.wait_ge(g_inv, t + 1)
                        dve.nop(nofuse=True)
                        nc.vector.tensor_scalar(qk[:, 0], qk[:, 0], inv[:, 0:1], None, ALU.mult)
                        nc.vector.tensor_scalar(qk[:, 1], qk[:, 1], inv[:, 1:2], None, ALU.mult) \
                            .then_inc(g_qks, 1)
                        dve.wait_ge(g_qkT, t + 1)
                        dve.nop(nofuse=True)
                        nc.vector.tensor_copy(qkT[:].rearrange("p a d -> p (a d)"), bank[4][:, 0:2 * D]) \
                            .then_inc(g_qkTc, 1)
                        dve.wait_ge(g_sv, t * 48 + 48)
                        dve.nop(nofuse=True)
                    else:
                        link(nc.vector.tensor_scalar(acc[:], acc[:], has[:], None, ALU.mult))
                        nc.vector.scalar_tensor_tensor(acc[:], H[:, t, :], hasnt[:], acc[:],
                                                       ALU.mult, ALU.add).then_inc(g_hp, 1)
                        dve.wait_ge(g_hp, T + t + 1)
                        dve.nop(nofuse=True)
                        nc.vector.tensor_tensor(acc[:], acc[:], H[:, t, :], ALU.add).then_inc(g_n2, 1)
                        dve.wait_ge(g_n2, T + t + 1)
                        dve.nop(nofuse=True)
                        with dve.If(t > 0):
                            dve.wait_ge(g_store, t * 16)
                            dve.nop(nofuse=True)
                        nc.vector.scalar_tensor_tensor(row_a[:], acc[:], 0.5, X[:, t, :],
                                                       ALU.mult, ALU.add).then_inc(g_out, 1)
                assert chain.links == LINKS, chain.links
                chain.count = start + T * LINKS

        FULL = 5
        FULL_B = 3

        def after(eng, semaphore, value):
            if isinstance(value, int):
                if value > 0:
                    eng.wait_ge(semaphore, value)
            else:
                eng.wait_ge(semaphore, value)
                eng.nop(nofuse=True)

        def steps(eng, lag, step, chain=None, links=0):
            first = lag + lag % 2
            for s in range(first):
                step(s, s % 2)
            turns = (T - first) // 2
            if chain:
                start = chain.count
            with eng.Fori(0, turns, 1) as i:
                if chain:
                    chain.repeated(i, start, 2 * links)
                step(i * 2 + first, 0)
                step(i * 2 + (first + 1), 1)
            if chain:
                assert chain.links == 2 * links, chain.links
                chain.count = start + turns * 2 * links
            for s in range(T, T + lag):
                step(s, s % 2)

        def due(s, lag):
            return not isinstance(s, int) or 0 <= s - lag < T

        def col(tile, t):
            return tile[:, bass.ds(t, 1)]

        words = packed[:].bitcast(F32)
        EXP_ROW = SLOTS + 3
        FIRST, SOURCE, LANE = SLOTS, SLOTS + 1, SLOTS + 2
        by_edge = [bank[p][:, 0:CHUNKS * EXP_ROW].rearrange("p (c k) -> p c k", k=EXP_ROW)
                   for p in range(2)]
        sums = [bank[p][:, 500:502] for p in range(2)]
        agg = [bank[2 + p][:, 0:D + 2] for p in range(2)]
        turned = [bank[4][:, p * D:(p + 1) * D] for p in range(2)]
        qku = [bank[5 + p][:, 0:3 * D] for p in range(2)]
        u_edge = [[bank[4 + 2 * p][:, c * D:(c + 1) * D] if c < 4 else bank[5 + 2 * p][:, 0:D]
                   for c in range(CHUNKS)] for p in range(2)]

        @block.sync
        def _(sp):
            for tile, source in ((w0_sb, w0), (wq_sb, wq), (wk_sb, wk)):
                sp.dma_start(tile[:], source).then_inc(w_loaded, 16)
            for c in range(2):
                sp.dma_start(a_sb[:, c:c + 1], a0[c * D:(c + 1) * D, :]).then_inc(w_loaded, 16)
            for c in range(4):
                sp.dma_start(X[:, c * CHUNK:(c + 1) * CHUNK, :],
                             xv[:, c * CHUNK:(c + 1) * CHUNK, :]).then_inc(x_loaded[c], 16)

            def load_adj(t, par):
                for h in range(2):
                    after(sp, half_packed, 2 * t - 4 + h + 1)
                    sp.dma_start(wide[:, par, h * (N // 2):(h + 1) * (N // 2)],
                                 adjv[t][:, h * (N // 2):(h + 1) * (N // 2)]) \
                        .then_inc(adj_loaded[par][h], 16)
            load_adj(0, 0)
            load_adj(1, 1)
            sp.wait_ge(zeroed, 1)
            for table in (rows0, rows1):
                sp.dma_start(table[0:1, :], zero_row[:]).then_inc(zero_stored, 16)

            def store_h(g, par):
                after(sp, h_staged, g + 1)
                after(sp, d_staged, g + 1)
                sp.dma_start(table0v[:, bass.ds(g * GROUP, GROUP), :], stage[:, par]) \
                    .then_inc(stored0[par], 16)
            pairs(sp, 0, GROUPS, store_h)

            def step(s, par):
                if not isinstance(s, int) or s + 2 < T:
                    load_adj(s + 2, par)
                if due(s, 5):
                    after(sp, row_staged, s - 5 + 1)
                    sp.dma_start(table1t[s - 5], stage[:, 1 - par, 0]).then_inc(stored1[1 - par], 16)
            for s in range(6):
                step(s, s % 2)
            with sp.Fori(0, (T - 8) // 2, 1) as i:
                step(i * 2 + 6, 0)
                step(i * 2 + 7, 1)
            for s in range(T - 2, T + 5):
                step(s, s % 2)
            for par in range(2):
                sp.wait_ge(stored1[par], 16 * T // 2)
            sp.wait_ge(flag_ready, 1)
            with sp.If(sp.value_load(flag[0:1, 0:1]) != 0):
                sp.wait_ge(u_ready, T)
                general_sync(sp)
            with sp.Else():
                def step_b(s, par):
                    if due(s, 3):
                        after(sp, b_out, s - 3 + 1)
                        sp.dma_start(outv[s - 3], hp[:, 1 - par]).then_inc(b_stored[1 - par], 16)
                steps(sp, FULL_B, step_b)
                for par in range(2):
                    sp.wait_ge(b_stored[par], 16 * T // 2)

        @block.gpsimd
        def _(pool):
            nc.gpsimd.memset(ident[:], 0.0).then_inc(consts, 1)
            nc.gpsimd.memset(ones[:], 1.0).then_inc(consts, 1)
            nc.gpsimd.memset(minus_half[:], -0.5).then_inc(consts, 1)
            nc.gpsimd.memset(stage[:], 1.0).then_inc(consts, 1)
            pool.wait_ge(consts, 4)
            nc.gpsimd.affine_select(out=ident[:], in_=ident[:], compare_op=ALU.not_equal, fill=1.0,
                                    base=0, pattern=[[-1, P]], channel_multiplier=1).then_inc(consts, 1)
            nc.gpsimd.memset(zero_row[:], 0.0).then_inc(zeroed, 1)
            nc.gpsimd.memset(base_bias[:], BASE).then_inc(sp_const, 1)
            nc.gpsimd.affine_select(out=tri[:], in_=ones[:], compare_op=ALU.is_gt, fill=0.0,
                                    base=0, pattern=[[1, P]], channel_multiplier=-1).then_inc(sp_const, 1)

            def iota(tile, pattern, base, multiplier):
                nc.gpsimd.iota(tile, pattern, base=base, channel_multiplier=multiplier,
                               allow_small_or_imprecise_dtypes=True).then_inc(sp_const, 1)
            iota(lane[:], [[1, P]], 0, 0)
            iota(edge_mid[:], [[1, EDGES]], 0, 0)
            iota(edge_no[:], [[P, CHUNKS]], 0, 1)
            iota(slot_no[:], [[1, SLOTS]], 0, 0)
            iota(seg_base[:], [[SEG, SEGS], [0, HITS]], 1, 0)
            iota(byte_base[:], [[WORDS, 4]], 0, 0)
            for par in range(2):
                iota(row_info[:, par, LANE:LANE + 1], [[0, 1]], 1, 1)

            def rsqrt_var(g, par):
                after(pool, var_ready, g + 1)
                nc.gpsimd.tensor_tensor(rstd[:, par], ve[:, par], minus_half[:], ALU.pow) \
                    .then_inc(rstd_ready, 1)
            pairs(pool, 0, GROUPS, rsqrt_var)
            pool.wait_ge(zero_stored, 32)
            for par in range(2):
                pool.wait_ge(stored0[par], 16 * GROUPS // 2)

            def gather(t, par, table, chunks):
                for c in chunks:
                    nc.gpsimd.indirect_dma_start(
                        out=G[:, par, c, :], out_offset=None, in_=table,
                        in_offset=bass.IndirectOffsetOnAxis(ap=gather_at[:, par, c:c + 1], axis=0)) \
                        .then_inc(gathered[par], 16)

            def step(s, par):
                if due(s, 3):
                    after(pool, listed, s - 3 + 1)
                    after(pool, collected, s - 5 + 1)
                    gather(s - 3, 1 - par, rows0, (0,))
                if due(s, 5):
                    after(pool, v_ready, s - 5 + 1)
                    nc.gpsimd.tensor_tensor(rs1[:], ve1[:], minus_half[:, 0:1], ALU.pow) \
                        .then_inc(r_ready, 1)
                if due(s, 3):
                    gather(s - 3, 1 - par, rows0, range(1, CHUNKS))
                if due(s, 5):
                    after(pool, norms_kept, s - 5 + 1)
                    nc.gpsimd.tensor_tensor(invs[:, 1 - par], n2s[:, 1 - par], minus_half[:, 0:2],
                                            ALU.pow).then_inc(inv_ready, 1)
            steps(pool, FULL, step)
            for par in range(2):
                pool.wait_ge(stored1[par], 16 * T // 2)
            pool.wait_ge(flag_ready, 1)
            with pool.If(pool.value_load(flag[0:1, 0:1]) != 0):
                general_gpsimd(pool)
            with pool.Else():
                def step_b(s, par):
                    if due(s, 1):
                        after(pool, b_at, s - 1 + 1)
                        after(pool, b_sum, s - 3 + 1)
                        gather(s - 1, 1 - par, rows1, range(CHUNKS))
                steps(pool, FULL_B, step_b)

        @block.scalar
        def _(act):
            def norm_relu(g, par):
                after(act, nmr_ready, g + 1)
                after(act, h0_turned, g - 1)
                for k in range(GROUP):
                    last = nc.scalar.activation(h0[:, par, k], X[:, g * GROUP + k, :], ACT.Relu,
                                                bias=nmr[:, par, k:k + 1], scale=rstd[:, par, k:k + 1])
                last.then_inc(h0_ready, 1)

            def stage_h(g, par):
                after(act, h_ready, g + 1)
                after(act, stored0[par], 8 * (g - par))
                after(act, mean_done, g - 1)
                nc.scalar.activation(stage[:, par, :, 0:D],
                                     bank[2 + par][:].rearrange("p (k d) -> p k d", d=D), ACT.Copy) \
                    .then_inc(h_staged, 1)

            def both(g, par):
                norm_relu(g, par)
                stage_h(g - 1, 1 - par)
            norm_relu(0, 0)
            act.wait_ge(consts, 5)
            both(1, 1)
            both(2, 0)
            pairs(act, 3, GROUPS - 1, both)
            both(GROUPS - 1, (GROUPS - 1) % 2)
            stage_h(GROUPS - 1, (GROUPS - 1) % 2)
            act.wait_ge(sp_const, 10)
            act.wait_ge(halved, 1)
            act.wait_ge(mean_done, GROUPS)
            for par in range(2):
                act.wait_ge(stored0[par], 16 * GROUPS // 2)

            def pack(s, par, g):
                if g % 2 == 0:
                    after(act, adj_loaded[par][g // 2], (s - par) * 8 + 16)
                source = wide[:, par, g * SEG:(g + 1) * SEG].rearrange("p (b w) -> p w b", b=4)
                made = nc.scalar.activation(packed[:, par, g].rearrange("p (w b) -> p w b", b=4), source,
                                            ACT.Identity, bias=base_bias[:],
                                            accum_out=entries[:, s, g:g + 1])
                if g % 2 == 1:
                    made.then_inc(half_packed, 1)

            def step(s, par):
                if due(s, 0):
                    after(act, searched, s - 1)
                    pack(s, par, 0)
                if due(s, 2):
                    after(act, mid_ready, s - 2 + 1)
                    after(act, spread_ready, s - 4 + 1)
                    nc.scalar.activation(away[:, par], edge_mid[:], ACT.Abs, bias=col(neg_mid, s - 2)) \
                        .then_inc(away_ready, 1)
                if due(s, 0):
                    pack(s, par, 1)
                if due(s, 4):
                    after(act, logit_ready, s - 4 + 1)
                    nc.scalar.activation(weight[:, par], logit[:, par], ACT.Exp).then_inc(weight_ready, 1)
                if due(s, 5):
                    after(act, m_ready, s - 5 + 1)
                    after(act, stored1[1 - par], (s - 5 - (1 - par)) * 8)
                    nc.scalar.activation(stage[:, 1 - par, 0, 0:D], X[:, s - 5, :], ACT.Relu,
                                         bias=nm1[:], scale=rs1[:]).then_inc(f_ready, 1)
                if due(s, 0):
                    pack(s, par, 2)
                if due(s, 5):
                    after(act, q_ready, s - 5 + 1)
                    for k in range(2):
                        last = nc.scalar.activation(unread[:, k], qku[1 - par][:, k * D:(k + 1) * D], ACT.Square,
                                                    accum_out=n2s[:, 1 - par, k:k + 1])
                    last.then_inc(norms_ready, 1)
                if due(s, 4):
                    after(act, rd_ready, s - 4 + 1)
                    nc.scalar.activation(hp[:, par], agg[par][:, 0:D], ACT.Copy, scale=rd[:, par:par + 1]) \
                        .then_inc(hp_ready, 1)
                if due(s, 0):
                    pack(s, par, 3)
                if due(s, 4):
                    after(act, min_ready, s - 4 + 1)
                    nc.scalar.activation(hmin[:, par], hmin[:, par], ACT.Exp).then_inc(exp_ready, 1)
                if due(s, 5):
                    after(act, inv_ready, s - 5 + 1)
                    nc.scalar.activation(H[:, s - 5, :], qku[1 - par][:, 2 * D:3 * D], ACT.Copy,
                                         scale=invs[:, 1 - par, 1:2]).then_inc(u_ready, 1)
            steps(act, FULL, step)
            act.wait_ge(flag_ready, 1)
            with act.If(act.value_load(flag[0:1, 0:1]) != 0):
                general_scalar(act)
            with act.Else():
                def step_b(s, par):
                    if due(s, 1):
                        after(act, b_spread, s - 3 + 1)
                        nc.scalar.activation(away[:, 1 - par], edge_mid[:], ACT.Abs,
                                             bias=col(neg_mid, s - 1)).then_inc(b_away, 1)
                    if due(s, 3):
                        after(act, b_rd, s - 3 + 1)
                        after(act, b_stored[1 - par], (s - 3 - (1 - par)) * 8)
                        nc.scalar.activation(hp[:, 1 - par], agg[1 - par][:, 0:D], ACT.Copy,
                                             scale=rd[:, 1 - par:2 - par]).then_inc(b_scaled, 1)
                    if due(s, 2):
                        after(act, b_dot, s - 2 + 1)
                        nc.scalar.activation(weight[:, par], logit[:, par], ACT.Exp).then_inc(b_weight, 1)
                steps(act, FULL_B, step_b)

        @block.tensor
        def _(pe):
            pe.wait_ge(w_loaded, 80)
            pe.wait_ge(consts, 5)
            nc.tensor.transpose(bank[4][:, 0:D], w0_sb[:], ident[:])
            nc.tensor.transpose(bank[4][:, D:2 * D], wq_sb[:], ident[:])
            nc.tensor.transpose(bank[4][:, 2 * D:3 * D], wk_sb[:], ident[:])
            nc.tensor.matmul(bank[4][:, 3 * D:4 * D], wk_sb[:], wq_sb[:], start=True, stop=True) \
                .then_inc(wT_ready, 1)
            pe.wait_ge(wT_copied, 1)
            nc.tensor.matmul(bank[5][:, 0:2], w0T[:], a_sb[:], start=True, stop=True) \
                .then_inc(wp_ready, 1)
            pe.wait_ge(wp_copied, 1)

            def turn_h0(g, par):
                after(pe, h0_ready, g + 1)
                after(pe, h0T_ready, g - 1)
                for k in range(GROUP):
                    last = nc.tensor.transpose(bank[par][:, k * D:(k + 1) * D], h0[:, par, k], ident[:])
                last.then_inc(h0_turned, 1)

            def project(g, par):
                after(pe, h0T_ready, g + 1)
                after(pe, h_staged, g - 1)
                after(pe, d_staged, g - 1)
                for k in range(GROUP):
                    left = h0T[:, par, k * D:(k + 1) * D]
                    nc.tensor.matmul(bank[2 + par][:, k * D:(k + 1) * D], left, w0_sb[:],
                                     start=True, stop=True)
                    last = nc.tensor.matmul(bank[4 + par][:, 2 * k:2 * k + 2], left, wa_sb[:],
                                            start=True, stop=True)
                last.then_inc(h_ready, 1)

            def add_mean(g, par, start=False, stop=False):
                after(pe, h_staged, g + 1)
                for k in range(GROUP):
                    last = nc.tensor.matmul(bank[7][:, 0:D], ones[:], stage[:, par, k, 0:D],
                                            start=start and k == 0, stop=stop and k == GROUP - 1)
                last.then_inc(mean_done, 1)

            turn_h0(0, 0)
            turn_h0(1, 1)
            project(0, 0)
            turn_h0(2, 0)
            project(1, 1)
            add_mean(0, 0, start=True)

            def both(g, par):
                turn_h0(g, par)
                project(g - 1, 1 - par)
                add_mean(g - 2, par)
            pairs(pe, 3, GROUPS - 1, both)
            both(GROUPS - 1, (GROUPS - 1) % 2)
            project(GROUPS - 1, (GROUPS - 1) % 2)
            add_mean(GROUPS - 2, GROUPS % 2)
            add_mean(GROUPS - 1, (GROUPS - 1) % 2, stop=True)
            pe.wait_ge(dmax_own, 1)
            nc.tensor.transpose(bank[6][0:1, 0:P], dmax_p[:], ident[:]).then_inc(dmax_turned, 1)
            pe.wait_ge(dmax_one, 1)
            nc.tensor.matmul(bank[6][:, 0:1], ones[0:1, :], denc[0:1, :], start=True, stop=True) \
                .then_inc(dmax_all, 1)
            pe.wait_ge(sp_const, 10)

            def step(s, par):
                if due(s, 2):
                    after(pe, counted, s - 2 + 1)
                    after(pe, listed, s - 4 + 1)
                    nc.tensor.matmul(sums[par][:, 0:1], tri[:], col(count, s - 2), start=True, stop=True)
                    nc.tensor.matmul(sums[par][:, 1:2], ones[:], col(count, s - 2), start=True, stop=True) \
                        .then_inc(summed, 1)
                    after(pe, spread_ready, s - 2 + 1)
                    for c in range(CHUNKS):
                        last = nc.tensor.matmul(by_edge[par][:, c], spread[:, par, c * P:(c + 1) * P],
                                                row_info[:, par], start=True, stop=True)
                    last.then_inc(spread_out, 1)
                if due(s, 5):
                    after(pe, f_ready, s - 5 + 1)
                    nc.tensor.transpose(turned[1 - par], stage[:, 1 - par, 0, 0:D], ident[:]) \
                        .then_inc(f_turned, 1)
                if due(s, 4):
                    after(pe, collect_ready, s - 4 + 1)
                    after(pe, hp_ready, s - 6 + 1)
                    for c in range(CHUNKS):
                        last = nc.tensor.matmul(agg[par], collect[:, par, c], G[:, par, c, 0:D + 2],
                                                start=(c == 0), stop=(c == CHUNKS - 1))
                    last.then_inc(collected, 1)
                if due(s, 5):
                    after(pe, fT_ready, s - 5 + 1)
                    after(pe, u_ready, s - 7 + 1)
                    nc.tensor.matmul(qku[1 - par], h2T[:], wqk[:].rearrange("p a d -> p (a d)"),
                                     start=True, stop=True).then_inc(q_ready, 1)
            steps(pe, FULL, step)
            pe.wait_ge(bad_ready, 1)
            nc.tensor.matmul(bank[7][:, 0:1], ones[:], bad_p[:], start=True, stop=True) \
                .then_inc(bad_all, 1)
            pe.wait_ge(flag_ready, 1)
            with pe.If(pe.value_load(flag[0:1, 0:1]) != 0):
                general_tensor(pe)
            with pe.Else():
                def step_b(s, par):
                    if due(s, 1):
                        after(pe, b_spread, s - 1 + 1)
                        after(pe, b_dot, s - 3 + 1)
                        for c in range(CHUNKS):
                            last = nc.tensor.matmul(u_edge[1 - par][c],
                                                    spread[:, 1 - par, c * P:(c + 1) * P],
                                                    H[:, s - 1, :], start=True, stop=True)
                        last.then_inc(b_u, 1)
                    if due(s, 2):
                        after(pe, b_collect, s - 2 + 1)
                        after(pe, b_scaled, s - 4 + 1)
                        for c in range(CHUNKS):
                            last = nc.tensor.matmul(agg[par], collect[:, par, c], G[:, par, c, 0:D + 2],
                                                    start=(c == 0), stop=(c == CHUNKS - 1))
                        last.then_inc(b_sum, 1)
                steps(pe, FULL_B, step_b)

        @block.vector
        def _(dve):
            chain = Chain(dve, dve_done)
            link = chain.link
            dve.wait_ge(wT_ready, 1)
            link(nc.vector.tensor_copy(wqk[:].rearrange("p a d -> p (a d)"), bank[4][:, D:4 * D]))
            nc.vector.tensor_copy(w0T[:], bank[4][:, 0:D]).then_inc(wT_copied, 1)
            dve.wait_ge(wp_ready, 1)
            nc.vector.tensor_copy(wa_sb[:], bank[5][:, 0:2]).then_inc(wp_copied, 1)
            FRONT = 2

            def moments(g, par):
                for k in range(GROUP):
                    last = nc.vector.bn_stats(stats[:, par, k], X[:, g * GROUP + k, :])
                link(last)
                for k in range(GROUP):
                    last = nc.vector.bn_aggr(mv[:, par, k], stats[:, par, k])
                link(last)
                nc.vector.tensor_scalar(ve[:, par], mv[:, par, :, 1], LN_EPS, None, ALU.add) \
                    .then_inc(var_ready, 1)

            def offsets(g, par):
                after(dve, rstd_ready, g + 1)
                nc.vector.scalar_tensor_tensor(nmr[:, par], mv[:, par, :, 0], -1.0, rstd[:, par],
                                               ALU.mult, ALU.mult).then_inc(nmr_ready, 1)

            def copy_h0T(g, par):
                after(dve, h0_turned, g + 1)
                after(dve, h_ready, g - 1)
                nc.vector.tensor_copy(h0T[:, par], bank[par][:]).then_inc(h0T_ready, 1)

            def stage_d(g, par):
                after(dve, h_ready, g + 1)
                after(dve, stored0[par], 8 * (g - par))
                both = bank[4 + par][:, 0:2 * GROUP].rearrange("p (k c) -> p k c", c=2)
                nc.vector.tensor_copy(src[:, bass.ds(g * GROUP, GROUP)], both[:, :, 0])
                nc.vector.tensor_copy(dst[:, bass.ds(g * GROUP, GROUP)], both[:, :, 1])
                nc.vector.tensor_copy(stage[:, par, :, D], both[:, :, 1]).then_inc(d_staged, 1)

            for c in range(4):
                dve.wait_ge(x_loaded[c], 16)
            dve.wait_ge(consts, 5)
            moments(0, 0)
            offsets(0, 0)
            moments(1, 1)
            offsets(1, 1)
            copy_h0T(0, 0)
            moments(2, 0)
            offsets(2, 0)
            copy_h0T(1, 1)
            stage_d(0, 0)
            start = chain.count - 3 * FRONT

            def front(g, par):
                chain.repeated(g, start, FRONT)
                moments(g, par)
                copy_h0T(g - 1, 1 - par)
                offsets(g, par)
                stage_d(g - 2, par)
            pairs(dve, 3, GROUPS - 1, front)
            front(GROUPS - 1, (GROUPS - 1) % 2)
            copy_h0T(GROUPS - 1, (GROUPS - 1) % 2)
            stage_d(GROUPS - 2, GROUPS % 2)
            stage_d(GROUPS - 1, (GROUPS - 1) % 2)
            chain.count = start + GROUPS * FRONT
            dve.wait_ge(d_staged, GROUPS)
            nc.vector.reduce_max(dmax_p[:], dst[:], AX.X).then_inc(dmax_own, 1)
            dve.wait_ge(dmax_turned, 1)
            nc.vector.reduce_max(denc[0:1, :], bank[6][0:1, 0:P], AX.X).then_inc(dmax_one, 1)
            dve.wait_ge(mean_done, GROUPS)
            link(nc.vector.tensor_scalar(mean_h[:], bank[7][:, 0:D], 1.0 / N, None, ALU.mult))
            dve.wait_ge(dmax_all, 1)
            link(nc.vector.tensor_copy(dst_max[:], bank[6][:, 0:1]))
            dve.wait_ge(sp_const, 10)
            nc.vector.tensor_scalar(edge_mid[:], edge_mid[:], 0.5, None, ALU.add).then_inc(halved, 1)

            def search(t, par, segs):
                for g in segs:
                    nc.vector.max_index(at[:, par, g], top[:, par, g], words[:, par, g])

            def decode(t, par):
                after(dve, searched, t + 1)
                link(nc.vector.scalar_tensor_tensor(at_base[:], at[:, par].rearrange("p g k -> p (g k)"), 1.0,
                                                    seg_base[:].rearrange("p g k -> p (g k)"),
                                                    ALU.mult, ALU.add))
                link(nc.vector.tensor_tensor(
                    cand_no[:], at_base[:].unsqueeze(2).broadcast_to([P, SEGS * HITS, 4]),
                    byte_base[:].unsqueeze(1).broadcast_to([P, SEGS * HITS, 4]), ALU.add))
                link(nc.vector.scalar_tensor_tensor(
                    cand[:], top[:, par].rearrange("p g k -> p (g k)").bitcast(U8), BASE + 1,
                    cand_no[:].rearrange("p w b -> p (w b)"), ALU.is_equal, ALU.mult))

            def compact(t, par):
                info = row_info[:, par]
                link(nc.vector.max(info[:, 0:8], cand[:]))
                link(nc.vector.match_replace(cand_b[:], info[:, 0:8], cand[:], 0.0))
                link(nc.vector.max(info[:, 8:16], cand_b[:]))
                link(nc.vector.tensor_scalar(used[:], info[:, 0:SLOTS], 0.0, None, ALU.is_gt))
                nc.vector.tensor_copy(info[:, SOURCE:SOURCE + 1], col(src, t))
                nc.vector.reduce_sum(col(count, t), used[:], AX.X).then_inc(counted, 1)

            def place_rows(t, par):
                after(dve, summed, t + 1)
                nc.vector.scalar_tensor_tensor(col(neg_mid, t), col(count, t), -0.5, sums[par][:, 0:1],
                                               ALU.mult, ALU.subtract).then_inc(mid_ready, 1)
                nc.vector.tensor_copy(row_info[:, par, FIRST:FIRST + 1], sums[par][:, 0:1])
                nc.vector.tensor_copy(col(total, t), sums[par][:, 1:2])
                link(nc.vector.tensor_scalar(col(reach, t), col(count, t), 0.5, -0.25, ALU.mult, ALU.add))

            def list_edges(t, par):
                after(dve, spread_out, t + 1)
                after(dve, gathered[par], (t - par) * (8 * CHUNKS))
                info = by_edge[par]
                link(nc.vector.tensor_tensor(nth[:], edge_no[:], info[:, :, FIRST], ALU.subtract))
                link(nc.vector.tensor_tensor(
                    pick[:], slot_no[:].unsqueeze(1).broadcast_to([P, CHUNKS, SLOTS]),
                    nth[:].unsqueeze(2).broadcast_to([P, CHUNKS, SLOTS]), ALU.is_equal))
                link(nc.vector.tensor_tensor(picked[:], pick[:], info[:, :, 0:SLOTS], ALU.mult))
                link(nc.vector.tensor_reduce(node_1[:], picked[:], AX.X, ALU.add))
                nc.vector.tensor_scalar(edge_node[:, t, :], node_1[:], 0.0, float(N), ALU.max, ALU.min)
                nc.vector.tensor_copy(edge_src[:, par], info[:, :, SOURCE])
                nc.vector.tensor_scalar(edge_row[:, t, :], info[:, :, LANE], -1.0, None, ALU.add)
                nc.vector.tensor_scalar(gather_at[:, par], node_1[:], 0.0, float(N), ALU.max, ALU.min) \
                    .then_inc(listed, 1)

            def shift_logits(t, par):
                after(dve, gathered[par], (t - par) * (8 * CHUNKS) + 16 * CHUNKS)
                nc.vector.tensor_tensor(z[:], edge_src[:, par], G[:, par, :, D], ALU.add)
                link(nc.vector.tensor_scalar(zm[:], edge_src[:, par], dst_max[:], None, ALU.add))
                nc.vector.scalar_tensor_tensor(lz[:], z[:], SLOPE, z[:], ALU.mult, ALU.max)
                link(nc.vector.scalar_tensor_tensor(lzm[:], zm[:], SLOPE, zm[:], ALU.mult, ALU.max))
                link(nc.vector.tensor_tensor(lg[:], lz[:], lzm[:], ALU.subtract))
                nc.vector.tensor_scalar(logit[:, par], lg[:], 0.0, None, ALU.min).then_inc(logit_ready, 1)

            def weigh(t, par, ready):
                for c in range(CHUNKS):
                    last = nc.vector.tensor_scalar(collect[:, par, c], lane[:], edge_row[:, t, c:c + 1],
                                                   weight[:, par, c:c + 1], ALU.is_equal, ALU.mult)
                last.then_inc(ready, 1)

            STEP = 24

            def step(s, par):
                odd = 1 - par
                if due(s, 5):
                    t = s - 5
                    after(dve, exp_ready, t + 1)
                    link(nc.vector.scalar_tensor_tensor(X[:, t, :], hmin[:, odd], -1.0, hsum[:],
                                                        ALU.add, ALU.add))
                    link(nc.vector.bn_stats(st1[:], X[:, t, :]))
                    link(nc.vector.bn_aggr(mv1[:], st1[:]))
                    nc.vector.tensor_scalar(ve1[:], mv1[:, 1:2], LN_EPS, None, ALU.add) \
                        .then_inc(v_ready, 1)
                if due(s, 2):
                    place_rows(s - 2, par)
                if due(s, 1):
                    after(dve, half_packed, 2 * (s - 1) + 1)
                    for g in (0, 1):
                        nc.vector.max(top[:, odd, g], words[:, odd, g])
                if due(s, 4):
                    shift_logits(s - 4, par)
                if due(s, 5):
                    after(dve, r_ready, s - 5 + 1)
                    nc.vector.scalar_tensor_tensor(nm1[:], mv1[:, 0:1], -1.0, rs1[:],
                                                   ALU.mult, ALU.mult).then_inc(m_ready, 1)
                if due(s, 1):
                    after(dve, half_packed, 2 * (s - 1) + 2)
                    nc.vector.max(top[:, odd, 2], words[:, odd, 2])
                    link(nc.vector.max(top[:, odd, 3], words[:, odd, 3]))
                if due(s, 2):
                    after(dve, away_ready, s - 2 + 1)
                    nc.vector.tensor_scalar(spread[:, par], away[:, par], col(reach, s - 2), None,
                                            ALU.is_le).then_inc(spread_ready, 1)
                if due(s, 4):
                    after(dve, weight_ready, s - 4 + 1)
                    weigh(s - 4, par, collect_ready)
                if due(s, 1):
                    search(s - 1, odd, (0, 1))
                if due(s, 5):
                    after(dve, f_turned, s - 5 + 1)
                    nc.vector.tensor_copy(h2T[:], turned[odd]).then_inc(fT_ready, 1)
                if due(s, 4):
                    after(dve, collected, s - 4 + 1)
                    link(nc.vector.tensor_scalar(denc[:], agg[par][:, D + 1:D + 2], TINY, None, ALU.max))
                    nc.vector.reciprocal(rd[:, par:par + 1], denc[:]).then_inc(rd_ready, 1)
                    link(nc.vector.tensor_scalar(lone[:, par:par + 1], col(count, s - 4), 0.0, None,
                                                 ALU.is_equal))
                    nc.vector.tensor_tensor(col(least, s - 4), denc[:], lone[:, par:par + 1], ALU.add)
                if due(s, 1):
                    search(s - 1, odd, (2,))
                    nc.vector.max_index(at[:, odd, 3], top[:, odd, 3], words[:, odd, 3]) \
                        .then_inc(searched, 1)
                if due(s, 2):
                    list_edges(s - 2, par)
                if due(s, 5):
                    after(dve, norms_ready, s - 5 + 1)
                    nc.vector.tensor_scalar(n2s[:, odd], n2s[:, odd], COS_EPS * COS_EPS, None, ALU.max) \
                        .then_inc(norms_kept, 1)
                if due(s, 1):
                    decode(s - 1, odd)
                if due(s, 4):
                    t = s - 4
                    after(dve, hp_ready, t + 1)
                    link(nc.vector.scalar_tensor_tensor(hp[:, par], mean_h[:], lone[:, par:par + 1],
                                                        hp[:, par], ALU.mult, ALU.add))
                    nc.vector.tensor_scalar(hmin[:, par], hp[:, par], 0.0, None, ALU.min) \
                        .then_inc(min_ready, 1)
                    link(nc.vector.scalar_tensor_tensor(hsum[:], hp[:, par], 0.0, X[:, t, :],
                                                        ALU.max, ALU.add))
                if due(s, 1):
                    compact(s - 1, odd)
                if due(s, 5):
                    t = s - 5
                    link(nc.vector.tensor_scalar(half_f[:, odd:odd + 1], lone[:, odd:odd + 1], 0.5, 0.5,
                                                 ALU.mult, ALU.add))
                    nc.vector.scalar_tensor_tensor(X[:, t, :], stage[:, odd, 0, 0:D], half_f[:, odd:odd + 1],
                                                   X[:, t, :], ALU.mult, ALU.add)
                    after(dve, inv_ready, t + 1)
                    nc.vector.tensor_copy(stage[:, odd, 0, D:D + 1], invs[:, odd, 0:1]) \
                        .then_inc(row_staged, 1)
            steps(dve, FULL, step, chain, STEP)

            dve.wait_ge(u_ready, T)
            link(nc.vector.tensor_reduce(chk[:], entries[:], AX.X, ALU.add))
            link(nc.vector.tensor_tensor(chk[:], chk[:], count[:], ALU.subtract))
            nc.vector.tensor_scalar(bad[:, 0], chk[:], BASE * N, None, ALU.not_equal)
            nc.vector.tensor_scalar(bad[:, 1], total[:], float(EDGES), None, ALU.is_gt)
            link(nc.vector.tensor_scalar(bad[:, 2], least[:], LEAST_SUM, None, ALU.is_lt))
            nc.vector.tensor_reduce(bad_p[:], bad[:], AX.XY, ALU.add).then_inc(bad_ready, 1)
            dve.wait_ge(bad_all, 1)
            nc.vector.tensor_copy(flag[:], bank[7][:, 0:1]).then_inc(flag_ready, 1)
            dve.wait_ge(flag_ready, 1)
            entry_count = chain.count
            with dve.If(dve.value_load(flag[0:1, 0:1]) != 0):
                general_vector(dve, chain)
            with dve.Else():
                chain.count = entry_count
                STEP_B = 2

                def step_b(s, par):
                    odd = 1 - par
                    if due(s, 0):
                        after(dve, gathered[par], 8 * CHUNKS * T + (s - par) * (8 * CHUNKS))
                        nc.vector.tensor_copy(gather_at[:, par], edge_node[:, s, :]).then_inc(b_at, 1)
                    if due(s, 1):
                        after(dve, b_away, s - 1 + 1)
                        after(dve, b_u, s - 3 + 1)
                        nc.vector.tensor_scalar(spread[:, odd], away[:, odd], col(reach, s - 1), None,
                                                ALU.is_le).then_inc(b_spread, 1)
                    if due(s, 3):
                        after(dve, b_sum, s - 3 + 1)
                        link(nc.vector.tensor_scalar(denc[:], agg[odd][:, D + 1:D + 2], TINY, 2.0,
                                                     ALU.max, ALU.mult))
                        nc.vector.reciprocal(rd[:, odd:odd + 1], denc[:]).then_inc(b_rd, 1)
                    if due(s, 2):
                        t = s - 2
                        after(dve, b_u, t + 1)
                        after(dve, gathered[par], 8 * CHUNKS * T + (t - par) * (8 * CHUNKS) + 16 * CHUNKS)
                        for c in range(CHUNKS):
                            last = nc.vector.tensor_tensor_reduce(
                                out=unread[:, c], in0=u_edge[par][c], in1=G[:, par, c, 0:D], scale=1.0, scalar=0.0,
                                op0=ALU.mult, op1=ALU.add, accum_out=lg[:, c:c + 1])
                        link(last)
                        nc.vector.tensor_tensor(logit[:, par], lg[:], G[:, par, :, D], ALU.mult) \
                            .then_inc(b_dot, 1)
                    if due(s, 3):
                        t = s - 3
                        after(dve, b_scaled, t + 1)
                        nc.vector.tensor_tensor(hp[:, odd], hp[:, odd], X[:, t, :], ALU.add) \
                            .then_inc(b_out, 1)
                    if due(s, 2):
                        after(dve, b_weight, s - 2 + 1)
                        weigh(s - 2, par, b_collect)
                steps(dve, FULL_B, step_b, chain, STEP_B)


def kernel(x, adj, L0_gnn_W, L0_gnn_a, L1_gnn_Wq, L1_gnn_Wk):
    import numpy as _np
    import concourse.bacc as _bacc
    from concourse import mybir as _mybir
    from concourse.bass_utils import run_bass_kernel_spmd as _run

    nc = _bacc.Bacc("TRN2", target_bir_lowering=False, num_devices=1)
    arrays, args = {}, []
    for name, a in (("x", x), ("adj", adj), ("w0", L0_gnn_W), ("a0", L0_gnn_a),
                    ("wq", L1_gnn_Wq), ("wk", L1_gnn_Wk)):
        a = _np.ascontiguousarray(a)
        arrays[f"in_{name}"] = a
        args.append(nc.dram_tensor(f"in_{name}", a.shape, _mybir.dt.from_np(a.dtype),
                                   kind="ExternalInput").ap())
    result = nc.dram_tensor("out_rows", (N, D), F32, kind="ExternalOutput")
    build(nc, *args, result.ap())
    r = _run(nc, [arrays], core_ids=[0])
    return r.results[0]["out_rows"]
```

```python
from contextlib import ExitStack

import numpy as np
import concourse.bass as bass
from concourse import mybir

N = 8192
D = 128
P = 128
T = N // P
ROW = 132
GROUP = 4
CB = 512
NB = N // CB
SEG = 2048
SEGS = N // SEG
WORDS = SEG // 4
HITS = 8
SLOTS = 16
CHUNKS = 5
EDGES = CHUNKS * P
BASE = 64.0
LEAST_SUM = 2.0 ** -40
OWN = 3
TINY = 2.0 ** -100
FIRST = SLOTS
LANE = SLOTS + 3
INFO = SLOTS + 4
XLOADS = 4
CONSTS = 8
LN_EPS = 1e-5
COS_EPS = 1e-4
SLOPE = 0.01
MASKED0 = 1e12
MASKED1 = 9e15

F32 = mybir.dt.float32
I32 = mybir.dt.int32
U32 = mybir.dt.uint32
U8 = mybir.dt.uint8
ALU = mybir.AluOpType
ACT = mybir.ActivationFunctionType
AX = mybir.AxisListType


class Chain:

    def __init__(self, engine, done):
        self.engine, self.done, self.count, self.links = engine, done, 0, 0

    def link(self, instruction):
        self.count = self.count + 1
        self.links += 1
        instruction.then_inc(self.done, 1)
        self.engine.wait_ge(self.done, self.count)
        if not isinstance(self.count, int):
            self.engine.nop(nofuse=True)

    def mark(self, instruction):
        self.count = self.count + 1
        self.links += 1
        instruction.then_inc(self.done, 1)

    def need(self, count):
        if not isinstance(count, int) or count:
            self.engine.wait_ge(self.done, count)
            if not isinstance(count, int):
                self.engine.nop(nofuse=True)

    def settle(self):
        self.need(self.count)

    def repeated(self, turn, before, each):
        self.count = turn * each + before
        self.links, self.each = 0, each


def build(nc, x, adj, w0, a0, wq, wk, out):
    ctx = ExitStack()
    with ctx:
        def sb(name, shape, dt=F32):
            return ctx.enter_context(nc.sbuf_tensor(name, shape, dt))

        def sem(name):
            return ctx.enter_context(nc.semaphore(name))

        def dram(name, shape):
            return nc.dram_tensor(name, shape, F32, kind="Internal").ap()

        rows0 = dram("rows0", (N + 1, ROW))
        rows1 = dram("rows1", (N + 1, ROW))
        table0, table1 = rows0[1:N + 1, :], rows1[1:N + 1, :]
        dst_row = dram("dst_row", (T, P))
        qn_cols = dram("qn_cols", (P, N))
        kn_cols = dram("kn_cols", (P, N))

        X = sb("X", [P, T, D])
        H = sb("H", [P, T, D])
        wide = sb("wide", [P, 2, N], I32)
        wide_a = wide[:, 0]
        wide_b = wide[:, 1].bitcast(F32)
        w0x = sb("w0x", [P, D + 2])
        w0T = sb("w0T", [P, D])
        a_sb = sb("a_sb", [P, 2])
        wq_sb = sb("wq_sb", [P, D])
        wk_sb = sb("wk_sb", [P, D])
        wqk = sb("wqk", [P, 3, D])
        ident = sb("ident", [P, P])
        ones = sb("ones", [P, P])
        minus_half = sb("minus_half", [P, GROUP])
        stats = sb("stats", [P, 2, GROUP, 6])
        mv = sb("mv", [P, 2, GROUP, 2])
        ve = sb("ve", [P, 2, GROUP])
        rstd = sb("rstd", [P, 2, GROUP])
        nmr = sb("nmr", [P, 2, GROUP])
        h0 = sb("h0", [P, 2, GROUP, D])
        h0T = sb("h0T", [P, 2, GROUP * D])
        stage = sb("stage", [P, 2, GROUP, ROW])
        dst = sb("dst", [P, T])
        dstT = sb("dstT", [T, P])
        spare0 = sb("spare0", [1, ROW])
        spare1 = sb("spare1", [1, ROW])
        h0_sum = sb("h0_sum", [P, GROUP * D])
        h0_col = sb("h0_col", [P, 1])
        source = sb("source", [P, T, 2])
        tri = sb("tri", [P, P])
        lane = sb("lane", [P, P])
        edge_mid = sb("edge_mid", [P, EDGES])
        edge_no = sb("edge_no", [P, CHUNKS])
        slot_no = sb("slot_no", [P, SLOTS])
        byte_column = sb("byte_column", [P, SEGS, HITS, 4])
        base_bias = sb("base_bias", [P, 1])
        dmax_1 = sb("dmax_1", [P, 1])
        dmax_p = sb("dmax_p", [P, 1])
        entries = sb("entries", [P, T, SEGS])
        count = sb("count", [P, T])
        total = sb("total", [P, T])
        least = sb("least", [P, T])
        neg_mid = sb("neg_mid", [P, T])
        reach = sb("reach", [P, T])
        edge_node = sb("edge_node", [P, T, CHUNKS], U32)
        edge_row = sb("edge_row", [P, T, CHUNKS])
        packed = sb("packed", [P, 2, SEGS, SEG], U8)
        top = sb("top", [P, 2, SEGS, HITS])
        at = sb("at", [P, 2, SEGS, HITS], U32)
        cand_no = sb("cand_no", [P, SEGS * HITS, 4])
        cand = sb("cand", [P, SEGS * HITS * 4])
        cand_b = sb("cand_b", [P, SEGS * HITS * 4])
        used = sb("used", [P, SLOTS])
        row_info = sb("row_info", [P, 2, INFO])
        count_1 = sb("count_1", [P, 2])
        away = sb("away", [P, 2, EDGES])
        spread = sb("spread", [P, 2, EDGES])
        nth = sb("nth", [P, CHUNKS])
        pick = sb("pick", [P, CHUNKS, SLOTS])
        picked = sb("picked", [P, CHUNKS, SLOTS])
        node_1 = sb("node_1", [P, CHUNKS])
        gather_at = sb("gather_at", [P, 2, CHUNKS], U32)
        edge_src = sb("edge_src", [P, 2, CHUNKS, 2])
        rows_now = sb("rows_now", [P, 2, CHUNKS - OWN])
        G = sb("G", [P, 2, CHUNKS, ROW])
        z = sb("z", [P, CHUNKS])
        lz = sb("lz", [P, CHUNKS])
        lg = sb("lg", [P, CHUNKS])
        logit = sb("logit", [P, 2, CHUNKS])
        weight = sb("weight", [P, 2, CHUNKS])
        collect = sb("collect", [P, 2, CHUNKS, P])
        denc = sb("denc", [P, 1])
        rd = sb("rd", [P, 2])
        hp = sb("hp", [P, 2, D])
        hmin = sb("hmin", [P, 2, D])
        hsum = sb("hsum", [P, 2, D])
        half_f = sb("half_f", [P, 1])
        half_1 = sb("half_1", [P, 1])
        bad = sb("bad", [P, 3, T])
        bad_p = sb("bad_p", [P, 1])
        chk = sb("chk", [P, T])
        flag = sb("flag", [P, 1], I32)
        unread = h0[:].rearrange("p a k d -> p (a k) d")
        n2s = sb("n2s", [P, 2, 2])
        invs = sb("invs", [P, 2, 2])
        kn_t = sb("kn_t", [P, P])
        qn_b = spread[:, 0, 0:CB]
        p_b = collect[:, 0, 0:4].rearrange("p c q -> p (c q)")
        pT = collect[:, 1, 0:4].rearrange("p c q -> p (c q)")
        acc = sb("acc", [P, D])
        rmax = sb("rmax", [P, 1])
        den = sb("den", [P, 1])
        rden = sb("rden", [P, 1])
        has = sb("has", [P, 1])
        hasnt = sb("hasnt", [P, 1])
        row_a = sb("row_a", [P, D])
        row_b = sb("row_b", [P, D])
        h2 = sb("h2", [P, D])
        h2T = sb("h2T", [P, D])
        n2 = sb("n2", [P, 2])
        inv = sb("inv", [P, 2])
        qk = sb("qk", [P, 2, D])
        qkT = sb("qkT", [P, 2, D])
        st1 = sb("st1", [P, 6])
        mv1 = sb("mv1", [P, 2])
        ve1 = sb("ve1", [P, 1])
        rs1 = sb("rs1", [P, 2])
        nm1 = sb("nm1", [P, 2])

        bank = [ctx.enter_context(nc.psum_tensor(f"bank{i}", [P, 512], F32)) for i in range(8)]

        x_loaded = [sem(f"x_loaded{c}") for c in range(4)]
        w_loaded = sem("w_loaded")
        consts = sem("consts")
        wT_ready = sem("wT_ready")
        wT_copied = sem("wT_copied")
        wp_ready = sem("wp_ready")
        wp_copied = sem("wp_copied")
        dve_done = sem("dve_done")
        var_ready = sem("var_ready")
        rstd_ready = sem("rstd_ready")
        nmr_ready = sem("nmr_ready")
        h0_ready = sem("h0_ready")
        h0_turned = sem("h0_turned")
        h0T_ready = sem("h0T_ready")
        h_ready = sem("h_ready")
        h_staged = sem("h_staged")
        stored0 = [sem(f"stored0_{i}") for i in range(2)]
        spare_ready = sem("spare_ready")
        spare_stored = sem("spare_stored")
        h0_added = sem("h0_added")
        mean_copied = sem("mean_copied")
        sources_kept = sem("sources_kept")
        rows_copied = sem("rows_copied")
        pool_collected = sem("pool_collected")
        counts_whole = sem("counts_whole")
        totals_ready = sem("totals_ready")
        sp_const = sem("sp_const")
        mean_done = sem("mean_done")
        halved = sem("halved")
        dmax_own = sem("dmax_own")
        dmax_turned = sem("dmax_turned")
        dmax_one = sem("dmax_one")
        dmax_all = sem("dmax_all")
        adj_loaded = [[sem(f"adj_loaded{p}{h}") for h in range(2)] for p in range(2)]
        segs_packed = sem("segs_packed")
        searched = sem("searched")
        counted = sem("counted")
        summed = sem("summed")
        mid_ready = sem("mid_ready")
        away_ready = sem("away_ready")
        spread_ready = sem("spread_ready")
        spread_out = sem("spread_out")
        listed = sem("listed")
        gathered = [sem(f"gathered{p}") for p in range(2)]
        logit_ready = sem("logit_ready")
        weight_ready = sem("weight_ready")
        collect_ready = sem("collect_ready")
        collected = sem("collected")
        rd_ready = sem("rd_ready")
        hp_ready = sem("hp_ready")
        min_ready = sem("min_ready")
        exp_ready = sem("exp_ready")
        v_ready = sem("v_ready")
        r_ready = sem("r_ready")
        m_ready = sem("m_ready")
        f_ready = sem("f_ready")
        f_turned = sem("f_turned")
        fT_ready = sem("fT_ready")
        q_ready = sem("q_ready")
        norms_ready = sem("norms_ready")
        norms_kept = sem("norms_kept")
        inv_ready = sem("inv_ready")
        u_ready = sem("u_ready")
        row_staged = sem("row_staged")
        stored1 = [sem(f"stored1_{p}") for p in range(2)]
        bad_ready = sem("bad_ready")
        bad_all = sem("bad_all")
        flag_ready = sem("flag_ready")
        b_at = sem("b_at")
        b_away = sem("b_away")
        b_spread = sem("b_spread")
        b_u = sem("b_u")
        b_dot = sem("b_dot")
        b_weight = sem("b_weight")
        b_collect = sem("b_collect")
        b_sum = sem("b_sum")
        b_gathered = [sem(f"b_gathered{b}") for b in range(4)]
        b_out = sem("b_out")
        b_stored = [sem(f"b_stored{p}") for p in range(2)]
        g_load = sem("g_load")
        g_row = sem("g_row")
        g_store = sem("g_store")
        g_dT = sem("g_dT")
        g_dTc = sem("g_dTc")
        g_kn = sem("g_kn")
        g_qb = sem("g_qb")
        g_adj = sem("g_adj")
        g_mm = sem("g_mm")
        g_mmc = sem("g_mmc")
        g_max = sem("g_max")
        g_exp = sem("g_exp")
        g_blk = sem("g_blk")
        g_pt = sem("g_pt")
        g_ptc = sem("g_ptc")
        g_pv = sem("g_pv")
        g_acc = sem("g_acc")
        g_hp = sem("g_hp")
        g_en = sem("g_en")
        g_ve = sem("g_ve")
        g_rs = sem("g_rs")
        g_h2 = sem("g_h2")
        g_h2T = sem("g_h2T")
        g_h2Tc = sem("g_h2Tc")
        g_qk = sem("g_qk")
        g_n2 = sem("g_n2")
        g_inv = sem("g_inv")
        g_qks = sem("g_qks")
        g_qkT = sem("g_qkT")
        g_qkTc = sem("g_qkTc")
        g_sv = sem("g_sv")
        g_out = sem("g_out")

        block = ctx.enter_context(nc.Block())

        xv = x.rearrange("(t p) d -> p t d", p=P)
        outv = out.rearrange("(t p) d -> t p d", p=P)
        adjv = adj.rearrange("(t p) n -> t p n", p=P)
        table0v = table0.rearrange("(t p) c -> p t c", p=P)
        table1v = table1.rearrange("(t p) c -> p t c", p=P)
        table1t = table1.rearrange("(t p) c -> t p c", p=P)
        GROUPS = T // GROUP
        CHUNK = T // 4

        def pairs(eng, first, last, step):
            with eng.Fori(0, (last - first) // 2, 1) as i:
                step(i * 2 + first, first % 2)
                step(i * 2 + (first + 1), (first + 1) % 2)

        def general_sync(sp):
            sp.wait_ge(g_dTc, 1)
            sp.nop(nofuse=True)
            sp.dma_start(dst_row, dstT[:]).then_inc(g_row, 16)
            sp.wait_ge(g_row, 16)
            sp.nop(nofuse=True)
            for layer in range(2):
                if layer == 0:
                    sp.dma_start(X[:], xv).then_inc(g_row, 16)
                    sp.wait_ge(g_row, 32)
                    sp.nop(nofuse=True)
                sp.dma_start(H[:], (table0v, table1v)[layer][:, :, 0:D]).then_inc(g_load, 16)
                with sp.Fori(0, T, 1) as t:
                    n = t + layer * T
                    with sp.If(n > 0):
                        sp.wait_ge(g_acc, n * NB)
                        sp.nop(nofuse=True)
                    sp.dma_start(wide_a, adjv[t]).then_inc(g_adj, 16)
                    if layer == 0:
                        sp.dma_start(wide_b, dst_row.rearrange("(o t) p -> o (t p)", o=1)
                                     .broadcast_to([P, N])).then_inc(g_kn, 16)
                        sp.wait_ge(g_h2, t + 1)
                        sp.nop(nofuse=True)
                        sp.dma_start(table1t[t][:, 0:D], h2[:]).then_inc(g_sv, 16)
                        sp.wait_ge(g_qkTc, t + 1)
                        sp.nop(nofuse=True)
                        sp.dma_start(qn_cols[:, bass.ds(t * P, P)], qkT[:, 0, :]).then_inc(g_sv, 16)
                        sp.dma_start(kn_cols[:, bass.ds(t * P, P)], qkT[:, 1, :]).then_inc(g_sv, 16)
                        sp.wait_ge(g_sv, t * 48 + 48)
                        sp.nop(nofuse=True)
                    else:
                        sp.dma_start(kn_t[:], kn_cols[:, bass.ds(t * P, P)]).then_inc(g_kn, 16)
                        with sp.Fori(0, NB, 1) as b:
                            with sp.If(t * NB + b > 0):
                                sp.wait_ge(g_mm, t * NB + b)
                                sp.nop(nofuse=True)
                            sp.dma_start(qn_b, qn_cols[:, bass.ds(b * CB, CB)]).then_inc(g_qb, 16)
                        sp.wait_ge(g_out, t + 1)
                        sp.nop(nofuse=True)
                        sp.dma_start(outv[t], row_a[:]).then_inc(g_store, 16)
                        sp.wait_ge(g_store, t * 16 + 16)
                        sp.nop(nofuse=True)

        def general_gpsimd(pool):
            with pool.Fori(0, T, 1) as t:
                pool.wait_ge(g_ve, t + 1)
                pool.nop(nofuse=True)
                nc.gpsimd.tensor_tensor(rs1[:, 0:1], ve1[:], minus_half[:, 0:1], ALU.pow).then_inc(g_rs, 1)
                pool.wait_ge(g_n2, t + 1)
                pool.nop(nofuse=True)
                nc.gpsimd.tensor_tensor(inv[:], n2[:], minus_half[:, 0:2], ALU.pow).then_inc(g_inv, 1)

        def general_scalar(act):
            for layer in range(2):
                with act.Fori(0, T, 1) as t:
                    n = t + layer * T
                    act.wait_ge(g_max, n + 1)
                    act.nop(nofuse=True)
                    nc.scalar.activation(wide_b, wide_b, ACT.Exp, bias=rmax[:],
                                         accum_out=den[:]).then_inc(g_exp, 1)
                    act.wait_ge(g_exp, n + 1)
                    act.nop(nofuse=True)
                    with act.Fori(0, NB, 1) as b:
                        with act.If(t * NB + b + layer * T * NB > 0):
                            act.wait_ge(g_pt, t * NB + b + layer * T * NB)
                            act.nop(nofuse=True)
                        nc.scalar.activation(p_b, wide_b[:, bass.ds(b * CB, CB)], ACT.Copy) \
                            .then_inc(g_blk, 1)
                    if layer == 0:
                        act.wait_ge(g_hp, t + 1)
                        act.nop(nofuse=True)
                        nc.scalar.activation(row_b[:], row_b[:], ACT.Exp).then_inc(g_en, 1)
                        act.wait_ge(g_rs, t + 1)
                        act.nop(nofuse=True)
                        act.wait_ge(nmr_ready, GROUPS + t + 1)
                        act.nop(nofuse=True)
                        nc.scalar.activation(h2[:], X[:, t, :], ACT.Relu, bias=nm1[:, 0:1],
                                             scale=rs1[:, 0:1]).then_inc(g_h2, 1)

        def general_tensor(pe):
            pe.wait_ge(sources_kept, GROUPS)
            pe.nop(nofuse=True)
            nc.tensor.transpose(bank[0][0:T, 0:P], dst[:], ident[:]).then_inc(g_dT, 1)
            pe.wait_ge(g_dTc, 1)
            pe.nop(nofuse=True)
            for layer in range(2):
                pe.wait_ge(g_load, 16 * layer + 16)
                pe.nop(nofuse=True)
                with pe.Fori(0, T, 1) as t:
                    n = t + layer * T
                    if layer == 1:
                        pe.wait_ge(g_kn, 16 * T + 16 * t + 16)
                        pe.nop(nofuse=True)
                        with pe.Fori(0, NB, 1) as b:
                            pe.wait_ge(g_qb, t * (16 * NB) + b * 16 + 16)
                            pe.nop(nofuse=True)
                            with pe.If(t * NB + b > 0):
                                pe.wait_ge(g_mmc, t * NB + b)
                                pe.nop(nofuse=True)
                            nc.tensor.matmul(bank[0][:], kn_t[:], qn_b, start=True, stop=True) \
                                .then_inc(g_mm, 1)
                    with pe.Fori(0, NB, 1) as b:
                        m = t * NB + b + layer * T * NB
                        pe.wait_ge(g_blk, m + 1)
                        pe.nop(nofuse=True)
                        for k in range(4):
                            last = nc.tensor.transpose(bank[1][:, k * P:(k + 1) * P],
                                                       p_b[:, k * P:(k + 1) * P], ident[:])
                        last.then_inc(g_pt, 1)
                        pe.wait_ge(g_ptc, m + 1)
                        pe.nop(nofuse=True)
                        for k in range(4):
                            last = nc.tensor.matmul(bank[2][:, 0:D], pT[:, k * P:(k + 1) * P],
                                                    H[:, b * 4 + k, :], start=(k == 0), stop=(k == 3))
                        last.then_inc(g_pv, 1)
                        pe.wait_ge(g_acc, m + 1)
                        pe.nop(nofuse=True)
                    if layer == 0:
                        pe.wait_ge(g_h2, t + 1)
                        pe.nop(nofuse=True)
                        nc.tensor.transpose(bank[3][:, 0:D], h2[:], ident[:]).then_inc(g_h2T, 1)
                        pe.wait_ge(g_h2Tc, t + 1)
                        pe.nop(nofuse=True)
                        nc.tensor.matmul(bank[3][:, 0:2 * D], h2T[:],
                                         wqk[:, 0:2, :].rearrange("p a d -> p (a d)"),
                                         start=True, stop=True).then_inc(g_qk, 1)
                        pe.wait_ge(g_qks, t + 1)
                        pe.nop(nofuse=True)
                        nc.tensor.transpose(bank[4][:, 0:D], qk[:, 0], ident[:])
                        nc.tensor.transpose(bank[4][:, D:2 * D], qk[:, 1], ident[:]).then_inc(g_qkT, 1)

        def general_vector(dve, chain):
            link = chain.link
            dve.wait_ge(g_dT, 1)
            dve.nop(nofuse=True)
            nc.vector.tensor_copy(dstT[:], bank[0][0:T, 0:P]).then_inc(g_dTc, 1)
            mask = wide_a.bitcast(F32)
            for layer in range(2):
                start = chain.count
                LINKS = (18, 11)[layer]
                with dve.Fori(0, T, 1) as t:
                    n = t + layer * T
                    chain.repeated(t, start, LINKS)
                    dve.wait_ge(g_adj, n * 16 + 16)
                    dve.nop(nofuse=True)
                    if layer == 0:
                        dve.wait_ge(g_kn, t * 16 + 16)
                        dve.nop(nofuse=True)
                        link(nc.vector.tensor_scalar(wide_b, wide_b, source[:, t, 0:1], None,
                                                     ALU.add))
                        link(nc.vector.scalar_tensor_tensor(wide_b, wide_b, SLOPE, wide_b,
                                                            ALU.mult, ALU.max))
                    else:
                        with dve.Fori(0, NB, 1) as b:
                            dve.wait_ge(g_mm, t * NB + b + 1)
                            dve.nop(nofuse=True)
                            nc.vector.tensor_copy(wide_b[:, bass.ds(b * CB, CB)], bank[0][:]) \
                                .then_inc(g_mmc, 1)
                        dve.wait_ge(g_mmc, t * NB + NB)
                        dve.nop(nofuse=True)
                        link(nc.vector.reduce_sum(has[:], wide_a, AX.X))
                        link(nc.vector.tensor_scalar(has[:], has[:], 0.0, None, ALU.is_gt))
                        link(nc.vector.tensor_scalar(hasnt[:], has[:], -1.0, 1.0, ALU.mult, ALU.add))
                    big = (MASKED0, MASKED1)[layer]
                    link(nc.vector.tensor_scalar(mask, wide_a, 0.0, None, ALU.is_gt))
                    link(nc.vector.tensor_tensor(wide_b, wide_b, mask, ALU.mult))
                    link(nc.vector.tensor_scalar(mask, mask, -1.0, big, ALU.add, ALU.mult))
                    link(nc.vector.tensor_tensor(wide_b, wide_b, mask, ALU.add))
                    nc.vector.tensor_reduce(rmax[:], wide_b, AX.X, ALU.max, negate=True) \
                        .then_inc(g_max, 1)
                    dve.wait_ge(g_exp, n + 1)
                    dve.nop(nofuse=True)
                    link(nc.vector.reciprocal(rden[:], den[:]))
                    link(nc.vector.memset(acc[:], 0.0))
                    with dve.Fori(0, NB, 1) as b:
                        m = t * NB + b + layer * T * NB
                        dve.wait_ge(g_pt, m + 1)
                        dve.nop(nofuse=True)
                        nc.vector.tensor_copy(pT, bank[1][:]).then_inc(g_ptc, 1)
                        dve.wait_ge(g_pv, m + 1)
                        dve.nop(nofuse=True)
                        nc.vector.tensor_tensor(acc[:], acc[:], bank[2][:, 0:D], ALU.add) \
                            .then_inc(g_acc, 1)
                        dve.wait_ge(g_acc, m + 1)
                        dve.nop(nofuse=True)
                    link(nc.vector.tensor_scalar(acc[:], acc[:], rden[:], None, ALU.mult))
                    if layer == 0:
                        nc.vector.tensor_scalar(row_b[:], acc[:], 0.0, None, ALU.min).then_inc(g_hp, 1)
                        link(nc.vector.scalar_tensor_tensor(acc[:], acc[:], 0.0, X[:, t, :],
                                                            ALU.max, ALU.add))
                        dve.wait_ge(g_en, t + 1)
                        dve.nop(nofuse=True)
                        link(nc.vector.scalar_tensor_tensor(X[:, t, :], row_b[:], -1.0, acc[:],
                                                            ALU.add, ALU.add))
                        link(nc.vector.bn_stats(st1[:], X[:, t, :]))
                        link(nc.vector.bn_aggr(mv1[:], st1[:]))
                        nc.vector.tensor_scalar(ve1[:], mv1[:, 1:2], LN_EPS, None, ALU.add) \
                            .then_inc(g_ve, 1)
                        dve.wait_ge(g_rs, t + 1)
                        dve.nop(nofuse=True)
                        nc.vector.scalar_tensor_tensor(nm1[:, 0:1], mv1[:, 0:1], -1.0, rs1[:, 0:1],
                                                       ALU.mult, ALU.mult).then_inc(nmr_ready, 1)
                        dve.wait_ge(g_h2T, t + 1)
                        dve.nop(nofuse=True)
                        nc.vector.tensor_copy(h2T[:], bank[3][:, 0:D]).then_inc(g_h2Tc, 1)
                        dve.wait_ge(g_qk, t + 1)
                        dve.nop(nofuse=True)
                        flat = qk[:].rearrange("p a d -> p (a d)")
                        link(nc.vector.tensor_copy(flat, bank[3][:, 0:2 * D]))
                        link(nc.vector.tensor_tensor(row_a[:], qk[:, 0], qk[:, 0], ALU.mult))
                        link(nc.vector.reduce_sum(n2[:, 0:1], row_a[:], AX.X))
                        link(nc.vector.tensor_tensor(row_a[:], qk[:, 1], qk[:, 1], ALU.mult))
                        link(nc.vector.reduce_sum(n2[:, 1:2], row_a[:], AX.X))
                        nc.vector.tensor_scalar(n2[:], n2[:], COS_EPS * COS_EPS, None, ALU.max) \
                            .then_inc(g_n2, 1)
                        dve.wait_ge(g_inv, t + 1)
                        dve.nop(nofuse=True)
                        nc.vector.tensor_scalar(qk[:, 0], qk[:, 0], inv[:, 0:1], None, ALU.mult)
                        nc.vector.tensor_scalar(qk[:, 1], qk[:, 1], inv[:, 1:2], None, ALU.mult) \
                            .then_inc(g_qks, 1)
                        dve.wait_ge(g_qkT, t + 1)
                        dve.nop(nofuse=True)
                        nc.vector.tensor_copy(qkT[:].rearrange("p a d -> p (a d)"), bank[4][:, 0:2 * D]) \
                            .then_inc(g_qkTc, 1)
                        dve.wait_ge(g_sv, t * 48 + 48)
                        dve.nop(nofuse=True)
                    else:
                        link(nc.vector.tensor_scalar(acc[:], acc[:], has[:], None, ALU.mult))
                        nc.vector.scalar_tensor_tensor(acc[:], H[:, t, :], hasnt[:], acc[:],
                                                       ALU.mult, ALU.add).then_inc(g_hp, 1)
                        dve.wait_ge(g_hp, T + t + 1)
                        dve.nop(nofuse=True)
                        nc.vector.tensor_tensor(acc[:], acc[:], H[:, t, :], ALU.add).then_inc(g_n2, 1)
                        dve.wait_ge(g_n2, T + t + 1)
                        dve.nop(nofuse=True)
                        with dve.If(t > 0):
                            dve.wait_ge(g_store, t * 16)
                            dve.nop(nofuse=True)
                        nc.vector.scalar_tensor_tensor(row_a[:], acc[:], 0.5, X[:, t, :],
                                                       ALU.mult, ALU.add).then_inc(g_out, 1)
                assert chain.links == LINKS, chain.links
                chain.count = start + T * LINKS

        LAGS = 8
        LAGS_B = 4
        DEEP = 4

        def after(eng, semaphore, value):
            if isinstance(value, int):
                if value > 0:
                    eng.wait_ge(semaphore, value)
            else:
                eng.wait_ge(semaphore, value)
                eng.nop(nofuse=True)

        def steps(eng, lags, step, unroll=2, chain=None, marks=0):
            first = lags + unroll
            for s in range(first):
                step(s, s % unroll)
            turns = (T - first) // unroll
            if chain:
                start = chain.count
            with eng.Fori(0, turns, 1) as i:
                if chain:
                    chain.repeated(i, start, unroll * marks)
                for n in range(unroll):
                    step(i * unroll + (first + n), n)
            if chain:
                assert chain.links == unroll * marks, chain.links
                chain.count = start + turns * unroll * marks
            for s in range(T, T + lags):
                step(s, s % unroll)

        def due(s, lag):
            return not isinstance(s, int) or 0 <= s - lag < T

        def draining(s):
            return isinstance(s, int) and s > T

        def col(tile, t):
            return tile[:, bass.ds(t, 1)]

        words = packed[:].bitcast(F32)

        def packed_row(par, g):
            return packed[:, par, bass.ds(g, 1), :].rearrange("p o (w b) -> p (o w) b", b=4)
        byte_no = byte_column[:].rearrange("p g k b -> p (g k) b")
        by_edge = [bank[p][:, 0:CHUNKS * INFO].rearrange("p (c k) -> p c k", k=INFO) for p in range(2)]
        before = [bank[p][:, 500:501] for p in range(2)]
        agg = [bank[2 + p][:, 0:D + 2] for p in range(2)]
        turned = bank[4][:, 0:D]
        qku = [bank[5 + p][:, 0:3 * D] for p in range(2)]
        u_edge = [[bank[4 + 2 * p][:, c * D:(c + 1) * D] if c < 4 else bank[5 + 2 * p][:, 0:D]
                   for c in range(CHUNKS)] for p in range(2)]
        GB = wide[:, 0].bitcast(F32)[:, 0:DEEP * CHUNKS * ROW] \
            .rearrange("p (b c r) -> p b c r", b=DEEP, c=CHUNKS)

        def lanes(k):
            return (2, k * (D + 2)) if k < 3 else (4, 0)

        @block.sync
        def _(sp):
            for tile, weights in ((w0x[:, 0:D], w0), (wq_sb[:], wq), (wk_sb[:], wk)):
                sp.dma_start(tile, weights).then_inc(w_loaded, 16)
            for c in range(2):
                sp.dma_start(a_sb[:, 1 - c:2 - c], a0[c * D:(c + 1) * D, :]).then_inc(w_loaded, 16)
            for c in range(XLOADS):
                sp.dma_start(X[:, c * CHUNK:(c + 1) * CHUNK, :],
                             xv[:, c * CHUNK:(c + 1) * CHUNK, :]).then_inc(x_loaded[c], 16)

            def load_half(t, par, h):
                after(sp, segs_packed, SEGS * (t - 2) + SEGS // 2 * (h + 1))
                sp.dma_start(wide[:, par, h * (N // 2):(h + 1) * (N // 2)],
                             adjv[t][:, h * (N // 2):(h + 1) * (N // 2)]).then_inc(adj_loaded[par][h], 16)

            def store_h(g, par):
                after(sp, h_staged, g + 1)
                sp.dma_start(table0v[:, bass.ds(g * GROUP, GROUP), :], stage[:, par]) \
                    .then_inc(stored0[par], 16)
            for g in range(GROUPS):
                store_h(g, g % 2)
                if g % 2:
                    load_half(g // 4, g // 4 % 2, g // 2 % 2)

            def step(s, par):
                if not isinstance(s, int) or 4 <= s + 2 < T:
                    load_half(s + 2, par, 0)
                    load_half(s + 2, par, 1)
                if due(s, 8):
                    after(sp, row_staged, s - 8 + 1)
                    sp.dma_start(table1t[s - 8], stage[:, par, 0]).then_inc(stored1[par], 16)
            sp.wait_ge(spare_ready, 2)
            sp.dma_start(rows0[0:1, :], spare0[:]).then_inc(spare_stored, 16)
            sp.dma_start(rows1[0:1, :], spare1[:]).then_inc(spare_stored, 16)
            for s in range(8):
                step(s, s % 2)
            with sp.Fori(0, (T - 10) // 2, 1) as i:
                step(i * 2 + 8, 0)
                step(i * 2 + 9, 1)
            for s in range(T - 2, T + LAGS):
                step(s, s % 2)
            for par in range(2):
                sp.wait_ge(stored1[par], 16 * T // 2)
            sp.wait_ge(flag_ready, 1)
            with sp.If(sp.value_load(flag[0:1, 0:1]) != 0):
                sp.wait_ge(u_ready, T)
                general_sync(sp)
            with sp.Else():
                def step_b(s, ph):
                    if due(s, 4):
                        after(sp, b_out, s - 4 + 1)
                        sp.dma_start(outv[s - 4], hp[:, ph % 2]).then_inc(b_stored[ph % 2], 16)
                steps(sp, LAGS_B, step_b, DEEP)
                for par in range(2):
                    sp.wait_ge(b_stored[par], 16 * T // 2)

        @block.gpsimd
        def _(pool):
            nc.gpsimd.memset(ident[:], 0.0).then_inc(consts, 1)
            nc.gpsimd.memset(ones[:], 1.0).then_inc(consts, 1)
            nc.gpsimd.memset(minus_half[:], -0.5).then_inc(consts, 1)
            nc.gpsimd.memset(base_bias[:], BASE).then_inc(consts, 1)
            nc.gpsimd.memset(stage[:], 1.0).then_inc(consts, 1)
            pool.wait_ge(consts, 5)
            nc.gpsimd.affine_select(out=ident[:], in_=ident[:], compare_op=ALU.not_equal, fill=1.0,
                                    base=0, pattern=[[-1, P]], channel_multiplier=1).then_inc(consts, 1)
            nc.gpsimd.memset(h0_sum[:], 0.0).then_inc(h0_added, 1)

            def rsqrt_var(g, par):
                after(pool, var_ready, g + 1)
                after(pool, h0_ready, g - 1)
                nc.gpsimd.tensor_tensor(rstd[:, par], ve[:, par], minus_half[:], ALU.pow) \
                    .then_inc(rstd_ready, 1)

            def add_h0(g, par):
                after(pool, h0_ready, g + 1)
                after(pool, h0_added, g + 1)
                nc.gpsimd.tensor_tensor(h0_sum[:], h0_sum[:], h0[:, par].rearrange("p k d -> p (k d)"),
                                        ALU.add).then_inc(h0_added, 1)

            def both(g, par):
                rsqrt_var(g, par)
                add_h0(g - 2, par)
            rsqrt_var(0, 0)
            rsqrt_var(1, 1)
            pairs(pool, 2, GROUPS, both)
            add_h0(GROUPS - 2, 0)
            add_h0(GROUPS - 1, 1)

            nc.gpsimd.affine_select(out=tri[:], in_=ones[:], compare_op=ALU.is_gt, fill=0.0,
                                    base=0, pattern=[[1, P]], channel_multiplier=-1).then_inc(sp_const, 1)

            def iota(tile, pattern, base, multiplier):
                nc.gpsimd.iota(tile, pattern, base=base, channel_multiplier=multiplier,
                               allow_small_or_imprecise_dtypes=True).then_inc(sp_const, 1)
            iota(lane[:], [[1, P]], 0, 0)
            iota(edge_mid[:], [[1, EDGES]], 0, 0)
            iota(edge_no[:], [[P, CHUNKS]], 0, 1)
            iota(slot_no[:], [[1, SLOTS]], 0, 0)
            iota(byte_column[:], [[SEG, SEGS], [0, HITS], [WORDS, 4]], 1, 0)
            for par in range(2):
                iota(row_info[:, par, LANE:LANE + 1], [[0, 1]], 1, 1)
            nc.gpsimd.memset(spare1[:, 0:D + 1], 0.0)
            nc.gpsimd.memset(spare1[:, D + 1:ROW], 1.0).then_inc(spare_ready, 1)

            def gather(buffer, ph, par, table, chunks, sems):
                for c in chunks:
                    nc.gpsimd.indirect_dma_start(
                        out=buffer[:, ph, c, :], out_offset=None, in_=table,
                        in_offset=bass.IndirectOffsetOnAxis(ap=gather_at[:, par, c:c + 1], axis=0)) \
                        .then_inc(sems[ph], 16)

            def step(s, par):
                odd = 1 - par
                if isinstance(s, int) and s == 4:
                    pool.wait_ge(spare_stored, 32)
                    for p in range(2):
                        pool.wait_ge(stored0[p], 16 * GROUPS // 2)
                if due(s, 4):
                    after(pool, listed, s - 4 + 1)
                    after(pool, collected, s - 6 + 1)
                    gather(G, par, par, rows0, (0, 1), gathered)
                if due(s, 7):
                    after(pool, v_ready, s - 7 + 1)
                    nc.gpsimd.tensor_tensor(rs1[:, odd:odd + 1], ve1[:], minus_half[:, 0:1], ALU.pow) \
                        .then_inc(r_ready, 1)
                if due(s, 4):
                    gather(G, par, par, rows0, (2,), gathered)
                if due(s, 5) and not draining(s):
                    after(pool, weight_ready, s - 5 + 1)
                    after(pool, rows_copied, s - 5 + 1)
                    after(pool, collected, s - 7 + 1)
                    for c in range(OWN, CHUNKS):
                        last = nc.gpsimd.tensor_scalar(
                            collect[:, odd, c], lane[:], rows_now[:, odd, c - OWN:c - OWN + 1],
                            weight[:, odd, c:c + 1], ALU.is_equal, ALU.mult)
                    last.then_inc(pool_collected, 1)
                if due(s, 4):
                    gather(G, par, par, rows0, (3, 4), gathered)
                if due(s, 8):
                    after(pool, norms_kept, s - 8 + 1)
                    nc.gpsimd.tensor_tensor(invs[:, par], n2s[:, par], minus_half[:, 0:2],
                                            ALU.pow).then_inc(inv_ready, 1)
            steps(pool, LAGS, step)
            for par in range(2):
                pool.wait_ge(stored1[par], 16 * T // 2)
            pool.wait_ge(flag_ready, 1)
            with pool.If(pool.value_load(flag[0:1, 0:1]) != 0):
                general_gpsimd(pool)
            with pool.Else():
                def step_b(s, ph):
                    if due(s, 1):
                        after(pool, b_at, s - 1 + 1)
                        after(pool, b_sum, s - 5 + 1)
                        gather(GB, (ph - 1) % DEEP, (ph - 1) % 2, rows1, range(CHUNKS), b_gathered)
                steps(pool, LAGS_B, step_b, DEEP)

        @block.scalar
        def _(act):
            def norm_relu(g, par):
                after(act, nmr_ready, g + 1)
                after(act, h0_turned, g - 1)
                after(act, h0_added, g)
                for k in range(GROUP):
                    last = nc.scalar.activation(h0[:, par, k], X[:, g * GROUP + k, :], ACT.Relu,
                                                bias=nmr[:, par, k:k + 1], scale=rstd[:, par, k:k + 1])
                last.then_inc(h0_ready, 1)

            def stage_h(g, par):
                after(act, h_ready, g + 1)
                after(act, sources_kept, g - 1)
                after(act, stored0[par], 8 * (g - par))
                nc.scalar.activation(stage[:, par, 0:3, 0:D + 1],
                                     bank[2 + par][:, 0:3 * (D + 2)]
                                     .rearrange("p (k d) -> p k d", k=3)[:, :, 0:D + 1], ACT.Copy)
                nc.scalar.activation(stage[:, par, 3, 0:D + 1], bank[4 + par][:, 0:D + 1], ACT.Copy) \
                    .then_inc(h_staged, 1)

            FREE = 8

            def both(g, par):
                stage_h(g - 2, par)
                norm_relu(g, par)
            norm_relu(0, 0)
            norm_relu(1, 1)
            act.wait_ge(consts, 6)
            both(2, 0)
            both(3, 1)
            pairs(act, 4, FREE, both)

            def pack_at(t, par, g):
                loaded = wide[:, par, bass.ds(g * SEG, SEG)].rearrange("p (b w) -> p w b", b=4)
                nc.scalar.activation(packed_row(par, g), loaded, ACT.Identity, bias=base_bias[:],
                                     accum_out=entries[:, t, bass.ds(g, 1)]).then_inc(segs_packed, 1)

            def pack(t, par, g):
                if g % 2 == 0:
                    after(act, adj_loaded[par][g // 2], (t - par) * 8 + 16)
                pack_at(t, par, g)

            for t in range(2):
                for h in range(2):
                    act.wait_ge(adj_loaded[t][h], 16)
                with act.Fori(0, SEGS // 2, 1) as i:
                    for n in range(2):
                        both(i * 2 + (FREE + SEGS * t + n), n)
                        pack_at(t, t, i * 2 + n)
            for g in range(FREE + 2 * SEGS, GROUPS):
                both(g, g % 2)
            stage_h(GROUPS - 2, 0)
            stage_h(GROUPS - 1, 1)

            def step(s, par):
                odd = 1 - par
                new = not isinstance(s, int) or 1 < s < T
                if isinstance(s, int) and s == 7:
                    for p in range(2):
                        act.wait_ge(stored0[p], 16 * GROUPS // 2)
                if isinstance(s, int) and s == 2:
                    act.wait_ge(halved, 1)
                if due(s, 8):
                    after(act, m_ready, s - 8 + 1)
                    after(act, stored1[par], (s - 8 - par) * 8)
                    nc.scalar.activation(stage[:, par, 0, 0:D], X[:, s - 8, :], ACT.Relu,
                                         bias=nm1[:, par:par + 1], scale=rs1[:, par:par + 1]) \
                        .then_inc(f_ready, 1)
                if new:
                    after(act, searched, s - 1)
                    pack(s, par, 0)
                if due(s, 6):
                    after(act, rd_ready, s - 6 + 1)
                    nc.scalar.activation(hp[:, par], agg[par][:, 0:D], ACT.Copy, scale=rd[:, par:par + 1]) \
                        .then_inc(hp_ready, 1)
                if new:
                    pack(s, par, 1)
                if due(s, 5):
                    after(act, logit_ready, s - 5 + 1)
                    nc.scalar.activation(weight[:, odd], logit[:, odd], ACT.Exp).then_inc(weight_ready, 1)
                if new:
                    pack(s, par, 2)
                if due(s, 2):
                    after(act, mid_ready, s - 2 + 1)
                    after(act, spread_ready, s - 4 + 1)
                    nc.scalar.activation(away[:, par], edge_mid[:], ACT.Abs, bias=col(neg_mid, s - 2)) \
                        .then_inc(away_ready, 1)
                if due(s, 8):
                    after(act, q_ready, s - 8 + 1)
                    for k in range(2):
                        last = nc.scalar.activation(unread[:, k], qku[par][:, k * D:(k + 1) * D], ACT.Square,
                                                    accum_out=n2s[:, par, k:k + 1])
                    last.then_inc(norms_ready, 1)
                if new:
                    pack(s, par, 3)
                if due(s, 6):
                    after(act, min_ready, s - 6 + 1)
                    nc.scalar.activation(hmin[:, par], hmin[:, par], ACT.Exp).then_inc(exp_ready, 1)
                if due(s, 8):
                    after(act, inv_ready, s - 8 + 1)
                    nc.scalar.activation(H[:, s - 8, :], qku[par][:, 2 * D:3 * D], ACT.Copy,
                                         scale=invs[:, par, 1:2]).then_inc(u_ready, 1)
            steps(act, LAGS, step)
            act.wait_ge(flag_ready, 1)
            with act.If(act.value_load(flag[0:1, 0:1]) != 0):
                general_scalar(act)
            with act.Else():
                def step_b(s, ph):
                    par = ph % 2
                    if due(s, 0):
                        after(act, b_spread, s - 2 + 1)
                        nc.scalar.activation(away[:, par], edge_mid[:], ACT.Abs,
                                             bias=col(neg_mid, s)).then_inc(b_away, 1)
                    if due(s, 2):
                        after(act, b_dot, s - 2 + 1)
                        nc.scalar.activation(weight[:, par], logit[:, par], ACT.Exp).then_inc(b_weight, 1)
                steps(act, LAGS_B, step_b, DEEP)

        @block.tensor
        def _(pe):
            pe.wait_ge(w_loaded, 80)
            pe.wait_ge(consts, 6)
            nc.tensor.transpose(bank[4][:, 0:D], w0x[:, 0:D], ident[:])
            nc.tensor.transpose(bank[4][:, D:2 * D], wq_sb[:], ident[:])
            nc.tensor.transpose(bank[4][:, 2 * D:3 * D], wk_sb[:], ident[:])
            nc.tensor.matmul(bank[4][:, 3 * D:4 * D], wk_sb[:], wq_sb[:], start=True, stop=True) \
                .then_inc(wT_ready, 1)
            pe.wait_ge(wT_copied, 1)
            nc.tensor.matmul(bank[5][:, 0:2], w0T[:], a_sb[:], start=True, stop=True) \
                .then_inc(wp_ready, 1)
            pe.wait_ge(wp_copied, 1)

            def turn_h0(g, par):
                after(pe, h0_ready, g + 1)
                after(pe, h0T_ready, g - 1)
                for k in range(GROUP):
                    last = nc.tensor.transpose(bank[par][:, k * D:(k + 1) * D], h0[:, par, k], ident[:])
                last.then_inc(h0_turned, 1)

            def project(g, par):
                after(pe, h0T_ready, g + 1)
                after(pe, sources_kept, g - 1)
                for k in range(GROUP):
                    b, c = lanes(k)
                    last = nc.tensor.matmul(bank[b + par][:, c:c + D + 2], h0T[:, par, k * D:(k + 1) * D],
                                            w0x[:], start=True, stop=True)
                last.then_inc(h_ready, 1)

            def both(g, par):
                project(g - 1, 1 - par)
                turn_h0(g, par)
            turn_h0(0, 0)
            both(1, 1)
            both(2, 0)
            both(3, 1)
            pairs(pe, 4, GROUPS, both)
            project(GROUPS - 1, (GROUPS - 1) % 2)
            pe.wait_ge(h0_added, GROUPS + 1)
            for k in range(GROUP):
                last = nc.tensor.matmul(bank[7][:, 0:1], h0_sum[:, k * D:(k + 1) * D], ones[:, 0:1],
                                        start=(k == 0), stop=(k == GROUP - 1))
            last.then_inc(mean_done, 1)
            pe.wait_ge(mean_copied, 1)
            nc.tensor.matmul(bank[7][0:1, 0:D], h0_col[:], w0x[:, 0:D], start=True, stop=True) \
                .then_inc(mean_done, 1)
            pe.wait_ge(dmax_own, 1)
            nc.tensor.transpose(bank[6][0:1, 0:P], dmax_p[:], ident[:]).then_inc(dmax_turned, 1)
            pe.wait_ge(dmax_one, 1)
            nc.tensor.matmul(bank[6][:, 0:1], ones[0:1, :], dmax_1[0:1, :], start=True, stop=True) \
                .then_inc(dmax_all, 1)
            pe.wait_ge(sp_const, CONSTS)

            def step(s, par):
                odd = 1 - par
                if due(s, 8):
                    after(pe, f_ready, s - 8 + 1)
                    nc.tensor.transpose(turned, stage[:, par, 0, 0:D], ident[:]).then_inc(f_turned, 1)
                if due(s, 2):
                    after(pe, counted, s - 2 + 1)
                    after(pe, listed, s - 4 + 1)
                    nc.tensor.matmul(before[par], tri[:], count_1[:, par:par + 1], start=True, stop=True) \
                        .then_inc(summed, 1)
                if due(s, 8):
                    after(pe, fT_ready, s - 8 + 1)
                    after(pe, u_ready, s - 10 + 1)
                    nc.tensor.matmul(qku[par], h2T[:], wqk[:].rearrange("p a d -> p (a d)"),
                                     start=True, stop=True).then_inc(q_ready, 1)
                if due(s, 5):
                    after(pe, collect_ready, s - 5 + 1)
                    if not draining(s):
                        after(pe, pool_collected, s - 5 + 1)
                    after(pe, hp_ready, s - 7 + 1)
                    for c in range(CHUNKS):
                        last = nc.tensor.matmul(agg[odd], collect[:, odd, c], G[:, odd, c, 0:D + 2],
                                                start=(c == 0), stop=(c == CHUNKS - 1))
                    last.then_inc(collected, 1)
                if due(s, 2):
                    after(pe, spread_ready, s - 2 + 1)
                    for c in range(CHUNKS):
                        last = nc.tensor.matmul(by_edge[par][:, c], spread[:, par, c * P:(c + 1) * P],
                                                row_info[:, par], start=True, stop=True)
                    last.then_inc(spread_out, 1)
            steps(pe, LAGS, step)
            pe.wait_ge(counts_whole, 1)
            nc.tensor.matmul(bank[7][:, 0:T], ones[:], total[:], start=True, stop=True) \
                .then_inc(totals_ready, 1)
            pe.wait_ge(bad_ready, 1)
            nc.tensor.matmul(bank[7][:, 0:1], ones[:], bad_p[:], start=True, stop=True) \
                .then_inc(bad_all, 1)
            pe.wait_ge(flag_ready, 1)
            with pe.If(pe.value_load(flag[0:1, 0:1]) != 0):
                general_tensor(pe)
            with pe.Else():
                def step_b(s, ph):
                    par, odd = ph % 2, 1 - ph % 2
                    if due(s, 1):
                        after(pe, b_spread, s - 1 + 1)
                        after(pe, b_dot, s - 3 + 1)
                        for c in range(CHUNKS):
                            last = nc.tensor.matmul(u_edge[odd][c], spread[:, odd, c * P:(c + 1) * P],
                                                    H[:, s - 1, :], start=True, stop=True)
                        last.then_inc(b_u, 1)
                    if due(s, 3):
                        after(pe, b_collect, s - 3 + 1)
                        after(pe, b_out, s - 5 + 1)
                        for c in range(CHUNKS):
                            last = nc.tensor.matmul(agg[odd], collect[:, odd, c],
                                                    GB[:, (ph - 3) % DEEP, c, 0:D + 2],
                                                    start=(c == 0), stop=(c == CHUNKS - 1))
                        last.then_inc(b_sum, 1)
                steps(pe, LAGS_B, step_b, DEEP)

        @block.vector
        def _(dve):
            chain = Chain(dve, dve_done)
            link, mark = chain.link, chain.mark
            dve.wait_ge(wT_ready, 1)
            link(nc.vector.tensor_copy(wqk[:].rearrange("p a d -> p (a d)"), bank[4][:, D:4 * D]))
            nc.vector.tensor_copy(w0T[:], bank[4][:, 0:D]).then_inc(wT_copied, 1)
            dve.wait_ge(wp_ready, 1)
            nc.vector.tensor_copy(w0x[:, D:D + 2], bank[5][:, 0:2]).then_inc(wp_copied, 1)

            def keep_sources(g, par):
                after(dve, h_staged, g + 1)
                nc.vector.tensor_copy(source[:, bass.ds(g * GROUP, 3), 0],
                                      bank[2 + par][:, 0:3 * (D + 2)]
                                      .rearrange("p (k d) -> p k d", k=3)[:, :, D + 1])
                nc.vector.tensor_copy(source[:, bass.ds(g * GROUP + 3, 1), 0], bank[4 + par][:, D + 1:D + 2])
                nc.vector.tensor_copy(dst[:, bass.ds(g * GROUP, GROUP)], stage[:, par, :, D]) \
                    .then_inc(sources_kept, 1)

            dve.wait_ge(consts, 6)

            def front(g, par):
                odd = 1 - par
                if isinstance(g, int) and g * GROUP % CHUNK == 0 and g < GROUPS:
                    dve.wait_ge(x_loaded[g * GROUP // CHUNK], 16)
                new = not isinstance(g, int) or g < GROUPS
                if new:
                    for k in range(GROUP):
                        last = nc.vector.bn_stats(stats[:, par, k], X[:, g * GROUP + k, :])
                    mark(last)
                if not isinstance(g, int) or 0 < g <= GROUPS:
                    after(dve, rstd_ready, g)
                    nc.vector.scalar_tensor_tensor(nmr[:, odd], mv[:, odd, :, 0], -1.0, rstd[:, odd],
                                                   ALU.mult, ALU.mult).then_inc(nmr_ready, 1)
                if not isinstance(g, int) or 1 < g <= GROUPS + 1:
                    after(dve, h0_turned, g - 1)
                    after(dve, h_ready, g - 3)
                    nc.vector.tensor_copy(h0T[:, par], bank[par][:]).then_inc(h0T_ready, 1)
                if new:
                    chain.settle()
                    for k in range(GROUP):
                        last = nc.vector.bn_aggr(mv[:, par, k], stats[:, par, k])
                    mark(last)
                if not isinstance(g, int) or g > 2:
                    keep_sources(g - 3, odd)
                if new:
                    chain.settle()
                    nc.vector.tensor_scalar(ve[:, par], mv[:, par, :, 1], LN_EPS, None, ALU.add) \
                        .then_inc(var_ready, 1)
            for g in range(4):
                front(g, g % 2)
            for c in range(1, XLOADS):
                dve.wait_ge(x_loaded[c], 16)
            start = chain.count
            with dve.Fori(0, (GROUPS - 4) // 2, 1) as i:
                chain.repeated(i, start, 4)
                front(i * 2 + 4, 0)
                front(i * 2 + 5, 1)
            assert chain.links == 4, chain.links
            chain.count = start + (GROUPS - 4) // 2 * 4
            def search_max(par, g):
                return nc.vector.max(top[:, par, g], words[:, par, g])

            def search_at(par, g):
                return nc.vector.max_index(at[:, par, g], top[:, par, g], words[:, par, g])

            dve.wait_ge(segs_packed, SEGS)
            front(GROUPS, 0)
            search_max(0, 0)
            search_max(0, 1)
            front(GROUPS + 1, 1)
            search_max(0, 2)
            mark(search_max(0, 3))
            front(GROUPS + 2, 0)
            dve.wait_ge(sources_kept, GROUPS)
            nc.vector.reduce_max(dmax_p[:], dst[:], AX.X).then_inc(dmax_own, 1)
            dve.wait_ge(mean_done, 1)
            nc.vector.tensor_scalar(h0_col[:], bank[7][:, 0:1], 1.0 / N, None, ALU.mult) \
                .then_inc(mean_copied, 1)
            chain.settle()
            search_at(0, 0)
            search_at(0, 1)
            dve.wait_ge(dmax_turned, 1)
            nc.vector.reduce_max(dmax_1[0:1, :], bank[6][0:1, 0:P], AX.X).then_inc(dmax_one, 1)
            search_at(0, 2)
            search_at(0, 3).then_inc(searched, 1)
            dve.wait_ge(mean_done, 2)
            link(nc.vector.memset(spare0[:, D:D + 1], 0.0))
            link(nc.vector.memset(spare0[:, D + 1:ROW], 1.0))
            nc.vector.tensor_copy(spare0[:, 0:D], bank[7][0:1, 0:D]).then_inc(spare_ready, 1)
            dve.wait_ge(dmax_all, 1)
            link(nc.vector.tensor_scalar(source[:, :, 1], source[:, :, 0], bank[6][:, 0:1], None, ALU.add))
            link(nc.vector.scalar_tensor_tensor(source[:, :, 1], source[:, :, 1], SLOPE, source[:, :, 1],
                                                ALU.mult, ALU.max))
            dve.wait_ge(sp_const, CONSTS)
            nc.vector.tensor_scalar(edge_mid[:], edge_mid[:], 0.5, None, ALU.add).then_inc(halved, 1)

            def weigh(t, par, chunks, ready):
                for c in chunks:
                    last = nc.vector.tensor_scalar(collect[:, par, c], lane[:], edge_row[:, t, c:c + 1],
                                                   weight[:, par, c:c + 1], ALU.is_equal, ALU.mult)
                last.then_inc(ready, 1)

            MARKS = 23

            def step(s, par):
                odd = 1 - par
                new = due(s, 1) and not (isinstance(s, int) and s == 1)
                info = row_info[:, par]
                chain.settle()
                if due(s, 7):
                    after(dve, exp_ready, s - 7 + 1)
                    mark(nc.vector.scalar_tensor_tensor(X[:, s - 7, :], hmin[:, odd], -1.0, hsum[:, odd],
                                                        ALU.add, ALU.add))
                if due(s, 2):
                    mark(nc.vector.max(info[:, 0:8], cand[:]))
                if due(s, 6):
                    after(dve, collected, s - 6 + 1)
                    mark(nc.vector.tensor_scalar(col(least, s - 6), agg[par][:, D + 1:D + 2], TINY, None,
                                                 ALU.max))
                if due(s, 5):
                    after(dve, gathered[odd], (s - 5 - odd) * (8 * CHUNKS) + 16 * CHUNKS)
                    mark(nc.vector.tensor_tensor(z[:], edge_src[:, odd, :, 0], G[:, odd, :, D], ALU.add))
                if new:
                    after(dve, segs_packed, SEGS * (s - 1) + 2)
                    search_max(odd, 0)
                chain.settle()
                if due(s, 6):
                    nc.vector.reciprocal(rd[:, par:par + 1], col(least, s - 6)).then_inc(rd_ready, 1)
                if due(s, 7):
                    mark(nc.vector.bn_stats(st1[:], X[:, s - 7, :]))
                if due(s, 5):
                    mark(nc.vector.scalar_tensor_tensor(lz[:], z[:], SLOPE, z[:], ALU.mult, ALU.max))
                if due(s, 2):
                    mark(nc.vector.match_replace(cand_b[:], info[:, 0:8], cand[:], 0.0))
                if new:
                    search_max(odd, 1)
                chain.settle()
                if due(s, 7):
                    mark(nc.vector.bn_aggr(mv1[:], st1[:]))
                if due(s, 5):
                    mark(nc.vector.tensor_tensor(lg[:], lz[:], edge_src[:, odd, :, 1], ALU.subtract))
                if due(s, 2):
                    mark(nc.vector.max(info[:, 8:16], cand_b[:]))
                if new:
                    after(dve, segs_packed, SEGS * (s - 1) + 4)
                    search_max(odd, 2)
                chain.settle()
                if due(s, 7):
                    nc.vector.tensor_scalar(ve1[:], mv1[:, 1:2], LN_EPS, None, ALU.add) \
                        .then_inc(v_ready, 1)
                if due(s, 5):
                    nc.vector.tensor_scalar(logit[:, odd], lg[:], 0.0, None, ALU.min) \
                        .then_inc(logit_ready, 1)
                if due(s, 2):
                    mark(nc.vector.tensor_scalar(used[:], info[:, 0:SLOTS], 0.0, None, ALU.is_gt))
                used_at = chain.count
                if new:
                    mark(search_max(odd, 3))
                tops_at = chain.count
                if due(s, 2):
                    chain.need(used_at)
                    mark(nc.vector.reduce_sum(col(count, s - 2), used[:], AX.X))
                if due(s, 8):
                    after(dve, f_turned, s - 8 + 1)
                    nc.vector.tensor_copy(h2T[:], turned).then_inc(fT_ready, 1)
                if due(s, 3):
                    after(dve, spread_out, s - 3 + 1)
                    mark(nc.vector.tensor_tensor(nth[:], edge_no[:], by_edge[odd][:, :, FIRST], ALU.subtract))
                if new:
                    chain.need(tops_at)
                    search_at(odd, 0)
                chain.settle()
                if due(s, 2):
                    nc.vector.tensor_scalar(count_1[:, par:par + 1], col(count, s - 2), 1.0, None, ALU.max) \
                        .then_inc(counted, 1)
                if due(s, 3):
                    mark(nc.vector.tensor_tensor(
                        pick[:], slot_no[:].unsqueeze(1).broadcast_to([P, CHUNKS, SLOTS]),
                        nth[:].unsqueeze(2).broadcast_to([P, CHUNKS, SLOTS]), ALU.is_equal))
                if due(s, 7):
                    after(dve, r_ready, s - 7 + 1)
                    nc.vector.scalar_tensor_tensor(nm1[:, odd:odd + 1], mv1[:, 0:1], -1.0,
                                                   rs1[:, odd:odd + 1], ALU.mult, ALU.mult) \
                        .then_inc(m_ready, 1)
                if new:
                    search_at(odd, 1)
                chain.settle()
                if due(s, 3):
                    mark(nc.vector.tensor_tensor(picked[:], pick[:], by_edge[odd][:, :, 0:SLOTS], ALU.mult))
                if due(s, 2):
                    t = s - 2
                    after(dve, summed, t + 1)
                    nc.vector.scalar_tensor_tensor(col(neg_mid, t), count_1[:, par:par + 1], -0.5,
                                                   before[par], ALU.mult, ALU.subtract) \
                        .then_inc(mid_ready, 1)
                    nc.vector.tensor_copy(info[:, FIRST:FIRST + 1], before[par])
                    nc.vector.tensor_copy(info[:, FIRST + 1:FIRST + 3], source[:, t, :])
                    mark(nc.vector.tensor_scalar(col(reach, t), count_1[:, par:par + 1], 0.5, -0.25,
                                                 ALU.mult, ALU.add))
                if due(s, 5):
                    after(dve, weight_ready, s - 5 + 1)
                    weigh(s - 5, odd, range(CHUNKS if draining(s) else OWN), collect_ready)
                chain.settle()
                if due(s, 3):
                    mark(nc.vector.tensor_reduce(node_1[:], picked[:], AX.X, ALU.add))
                if new:
                    search_at(odd, 2)
                chain.settle()
                if due(s, 3):
                    t = s - 3
                    after(dve, gathered[odd], (t - odd) * (8 * CHUNKS))
                    nc.vector.tensor_scalar(edge_node[:, t, :], node_1[:], 0.0, float(N), ALU.max, ALU.min)
                    nc.vector.tensor_copy(edge_src[:, odd], by_edge[odd][:, :, FIRST + 1:FIRST + 3])
                    nc.vector.tensor_scalar(edge_row[:, t, :], by_edge[odd][:, :, LANE], -1.0, None, ALU.add)
                    nc.vector.tensor_scalar(gather_at[:, odd], node_1[:], 0.0, float(N), ALU.max, ALU.min) \
                        .then_inc(listed, 1)
                if due(s, 8):
                    after(dve, norms_ready, s - 8 + 1)
                    nc.vector.tensor_scalar(n2s[:, par], n2s[:, par], COS_EPS * COS_EPS, None, ALU.max) \
                        .then_inc(norms_kept, 1)
                if new:
                    search_at(odd, 3).then_inc(searched, 1)
                if due(s, 6):
                    after(dve, hp_ready, s - 6 + 1)
                    nc.vector.tensor_scalar(hmin[:, par], hp[:, par], 0.0, None, ALU.min) \
                        .then_inc(min_ready, 1)
                    mark(nc.vector.scalar_tensor_tensor(hsum[:, par], hp[:, par], 0.0, X[:, s - 6, :],
                                                        ALU.max, ALU.add))
                if due(s, 8):
                    mark(nc.vector.tensor_scalar(half_f[:], col(count, s - 8), 0.0, 0.5,
                                                 ALU.is_equal, ALU.mult))
                half_at = chain.count
                if due(s, 1):
                    after(dve, searched, s)
                    mark(nc.vector.tensor_tensor(
                        cand_no[:], at[:, odd].rearrange("p g k -> p (g k)").unsqueeze(2)
                        .broadcast_to([P, SEGS * HITS, 4]), byte_no, ALU.add))
                if due(s, 2):
                    after(dve, away_ready, s - 2 + 1)
                    nc.vector.tensor_scalar(spread[:, par], away[:, par], col(reach, s - 2), None,
                                            ALU.is_le).then_inc(spread_ready, 1)
                if due(s, 8):
                    chain.need(half_at)
                    mark(nc.vector.tensor_scalar(half_1[:], half_f[:], 0.5, None, ALU.add))
                half_at = chain.count
                if due(s, 1):
                    chain.settle()
                    mark(nc.vector.scalar_tensor_tensor(
                        cand[:], top[:, odd].rearrange("p g k -> p (g k)").bitcast(U8), BASE + 1,
                        cand_no[:].rearrange("p w b -> p (w b)"), ALU.is_equal, ALU.mult))
                if due(s, 4) and not draining(s + 1):
                    nc.vector.tensor_copy(rows_now[:, par], edge_row[:, s - 4, OWN:CHUNKS]) \
                        .then_inc(rows_copied, 1)
                if due(s, 8):
                    chain.need(half_at)
                    nc.vector.scalar_tensor_tensor(X[:, s - 8, :], stage[:, par, 0, 0:D], half_1[:],
                                                   X[:, s - 8, :], ALU.mult, ALU.add)
                    after(dve, inv_ready, s - 8 + 1)
                    nc.vector.tensor_copy(stage[:, par, 0, D:D + 1], invs[:, par, 0:1]) \
                        .then_inc(row_staged, 1)
            steps(dve, LAGS, step, 2, chain, MARKS)

            nc.vector.tensor_scalar(total[:], count[:], 1.0, None, ALU.max).then_inc(counts_whole, 1)
            dve.wait_ge(u_ready, T)
            link(nc.vector.tensor_reduce(chk[:], entries[:], AX.X, ALU.add))
            link(nc.vector.tensor_tensor(chk[:], chk[:], count[:], ALU.subtract))
            nc.vector.tensor_scalar(bad[:, 0], chk[:], BASE * N, None, ALU.not_equal)
            dve.wait_ge(totals_ready, 1)
            nc.vector.tensor_scalar(bad[:, 1], bank[7][:, 0:T], float(EDGES), None, ALU.is_gt)
            link(nc.vector.tensor_scalar(bad[:, 2], least[:], LEAST_SUM, None, ALU.is_lt))
            nc.vector.tensor_reduce(bad_p[:], bad[:], AX.XY, ALU.add).then_inc(bad_ready, 1)
            dve.wait_ge(bad_all, 1)
            nc.vector.tensor_copy(flag[:], bank[7][:, 0:1]).then_inc(flag_ready, 1)
            dve.wait_ge(flag_ready, 1)
            entry_count = chain.count
            with dve.If(dve.value_load(flag[0:1, 0:1]) != 0):
                general_vector(dve, chain)
            with dve.Else():
                chain.count = entry_count
                MARKS_B = 3

                def step_b(s, ph):
                    par, odd = ph % 2, 1 - ph % 2
                    if due(s, 0):
                        after(dve, b_gathered[(ph - 2) % DEEP],
                              (s - 2 - (ph - 2) % DEEP) * (16 * CHUNKS // DEEP) + 16 * CHUNKS
                              if not isinstance(s, int) or s >= 2 else 0)
                        nc.vector.tensor_copy(gather_at[:, par], edge_node[:, s, :]).then_inc(b_at, 1)
                    if due(s, 1):
                        after(dve, b_away, s - 1 + 1)
                        nc.vector.tensor_scalar(spread[:, odd], away[:, odd], col(reach, s - 1), None,
                                                ALU.is_le).then_inc(b_spread, 1)
                    if due(s, 4):
                        after(dve, b_sum, s - 4 + 1)
                        mark(nc.vector.tensor_scalar(denc[:], agg[par][:, D + 1:D + 2], 2.0, None, ALU.mult))
                    twice_at = chain.count
                    if due(s, 3):
                        after(dve, b_weight, s - 3 + 1)
                        weigh(s - 3, odd, range(CHUNKS), b_collect)
                    if due(s, 4):
                        chain.need(twice_at)
                        mark(nc.vector.reciprocal(rd[:, par:par + 1], denc[:]))
                    rd_at = chain.count
                    if due(s, 2):
                        t, b = s - 2, (ph - 2) % DEEP
                        after(dve, b_u, t + 1)
                        after(dve, b_gathered[b], (t - b) * (16 * CHUNKS // DEEP) + 16 * CHUNKS)
                        for c in range(CHUNKS):
                            last = nc.vector.tensor_tensor_reduce(
                                out=unread[:, c], in0=u_edge[par][c], in1=GB[:, b, c, 0:D], scale=1.0,
                                scalar=0.0, op0=ALU.mult, op1=ALU.add, accum_out=lg[:, c:c + 1])
                        mark(last)
                    if due(s, 4):
                        chain.need(rd_at)
                        after(dve, b_stored[par], (s - 4 - par) * 8)
                        nc.vector.scalar_tensor_tensor(hp[:, par], agg[par][:, 0:D], rd[:, par:par + 1],
                                                       X[:, s - 4, :], ALU.mult, ALU.add).then_inc(b_out, 1)
                    if due(s, 2):
                        chain.settle()
                        nc.vector.tensor_tensor(logit[:, par], lg[:], GB[:, b, :, D], ALU.mult) \
                            .then_inc(b_dot, 1)
                steps(dve, LAGS_B, step_b, DEEP, chain, MARKS_B)


def kernel(x, adj, L0_gnn_W, L0_gnn_a, L1_gnn_Wq, L1_gnn_Wk):
    import numpy as _np
    import concourse.bacc as _bacc
    from concourse import mybir as _mybir
    from concourse.bass_utils import run_bass_kernel_spmd as _run

    nc = _bacc.Bacc("TRN2", target_bir_lowering=False, num_devices=1)
    arrays, args = {}, []
    for name, a in (("x", x), ("adj", adj), ("w0", L0_gnn_W), ("a0", L0_gnn_a),
                    ("wq", L1_gnn_Wq), ("wk", L1_gnn_Wk)):
        a = _np.ascontiguousarray(a)
        arrays[f"in_{name}"] = a
        args.append(nc.dram_tensor(f"in_{name}", a.shape, _mybir.dt.from_np(a.dtype),
                                   kind="ExternalInput").ap())
    result = nc.dram_tensor("out_rows", (N, D), F32, kind="ExternalOutput")
    build(nc, *args, result.ap())
    r = _run(nc, [arrays], core_ids=[0])
    return r.results[0]["out_rows"]
```
